# Optimizing a Trainium2 kernel written in Bass

```python
import numpy as np
import jax
import jax.numpy as jnp

def _softmax(x, axis=-1):
    return jax.nn.softmax(x, axis=axis)

def _gelu(x):
    return jax.nn.gelu(x, approximate=True)

def _silu(x):
    return jax.nn.silu(x)

def _sigmoid(x):
    return jax.nn.sigmoid(x)

def _layernorm(x, axis=-1, eps=1e-05):
    m = jnp.mean(x, axis=axis, keepdims=True)
    v = jnp.var(x, axis=axis, keepdims=True)
    return (x - m) / jnp.sqrt(v + eps)

def _scatter_add(tgt, idx, src, axis=0):
    return tgt.at[idx].add(src)

def _segment_sum(src, seg, n):
    return jax.ops.segment_sum(src, seg, n)
kernel_name = 'mk_flamingo_gated_d1_seqx_r2_a41320'

def setup_inputs(seed: int=0):
    np.random.seed(seed)
    _w = jnp.asarray

    def _rec_inputs():
        import jax
        import jax.numpy as jnp
        _rk = jax.random.key(seed)
        x = -7.109e-05 + 0.9999 * jax.random.normal(jax.random.fold_in(_rk, 1), (8, 100, 2048), jnp.float32)
        _lenS = 100 - jax.random.randint(jax.random.fold_in(_rk, 7), (8,), 0, max(1, 100 // 4) + 1, jnp.int32)
        _lenS2 = 722 - jax.random.randint(jax.random.fold_in(_rk, 8), (8,), 0, max(1, 722 // 4) + 1, jnp.int32)
        _ctx_4096P = jax.random.normal(jax.random.fold_in(_rk, 11), (8, 16, 2048), jnp.float32)
        _ctx_4096c = jax.random.dirichlet(jax.random.fold_in(_rk, 511), 0.3 * jnp.ones((16,), jnp.float32), (8, 722))
        _ctx_4096t = jnp.einsum('bsk,bkd->bsd', _ctx_4096c, _ctx_4096P)
        _ctx_4096t = _ctx_4096t * jax.lax.rsqrt(jnp.mean(jnp.square(_ctx_4096t)) + 1e-12) * 0.953939
        ctx_4096 = -0.00010331 + 0.999899 * (_ctx_4096t + 0.3 * jax.random.normal(jax.random.fold_in(_rk, 611), (8, 722, 2048), jnp.float32))
        _g = jax.random.normal(jax.random.fold_in(_rk, 9001), (2, 1), jnp.float32)
        _g = jnp.sign(_g) * jnp.maximum(jnp.abs(_g), 1.0) + (_g == 0) * 1.0
        g_xattn = _g[0]
        g_ffn = _g[1]
        return (x, ctx_4096, g_xattn, g_ffn)
    x, ctx_4096, g_xattn, g_ffn = _rec_inputs()

    def _L0_xattn_setup():
        import jax, jax.numpy as jnp
        import numpy as np
        key = jax.random.key(seed)
        k1, k2 = jax.random.split(key)
        B, Lq, Lk, D = (16, 512, 1024, 2048)
        query = jax.random.normal(k1, (B, Lq, D), dtype=jnp.float32)
        key_t = jax.random.normal(k2, (B, Lk, D), dtype=jnp.float32)
        return {'query': query, 'key': key_t}
    _L0_xattn_all = _L0_xattn_setup()
    _L0_xattn_in = {k: v for k, v in _L0_xattn_all.items() if k in ()}
    del _L0_xattn_all

    def _L0_ffn_setup():
        import jax, jax.numpy as jnp
        import numpy as np
        IN_FEATURES = 2048

        def _dequantize(qweight, scale, zero_point):
            N, K_packed = qweight.shape
            groups = K_packed // 3
            p = qweight.reshape(N, groups, 3)
            v0 = p[:, :, 0] & 63
            v1 = p[:, :, 0] >> 6 & 63
            v2 = p[:, :, 1] & 63
            v3 = p[:, :, 2] & 63
            unpacked = jnp.stack([v0, v1, v2, v3], axis=2).reshape(N, groups * 4)
            unpacked = unpacked[:, :IN_FEATURES]
            return (unpacked.astype(jnp.float32) - zero_point) * scale
        key = jax.random.key(seed)
        k1, k2, k3, k4, k5 = jax.random.split(key, 5)
        x = jax.random.normal(k1, (8, 1024, 2048), dtype=jnp.float32)
        qweight = jax.random.randint(k2, (2048, 1536), 0, 2048, dtype=jnp.int32)
        weight_scale = jax.random.uniform(k3, (2048, 1), dtype=jnp.float32) * 0.02 + 0.001
        weight_zero_point = jax.random.uniform(k4, (2048, 1), dtype=jnp.float32) * 63.0
        bias = jax.random.normal(k5, (2048,), dtype=jnp.float32)
        return {'x': x, 'qweight': qweight, 'weight_scale': weight_scale, 'weight_zero_point': weight_zero_point, 'bias': bias}
    _L0_ffn_all = _L0_ffn_setup()
    _L0_ffn_in = {k: v for k, v in _L0_ffn_all.items() if k in ('qweight', 'weight_scale', 'weight_zero_point', 'bias')}
    del _L0_ffn_all
    return {'x': x, 'ctx_4096': ctx_4096, 'g_xattn': g_xattn, 'g_ffn': g_ffn, 'L0_ffn_qweight': _L0_ffn_in['qweight'], 'L0_ffn_weight_scale': _L0_ffn_in['weight_scale'], 'L0_ffn_weight_zero_point': _L0_ffn_in['weight_zero_point'], 'L0_ffn_bias': _L0_ffn_in['bias']}

def reference(x, ctx_4096, g_xattn, g_ffn, L0_ffn_qweight, L0_ffn_weight_scale, L0_ffn_weight_zero_point, L0_ffn_bias):
    import jax
    import jax.numpy as jnp

    def _L0_xattn_ref(query, key):
        import jax, jax.numpy as jnp
        import numpy as np
        a = jnp.einsum('bqd,bkd->bqk', query, key)
        e = jax.nn.softmax(a, axis=-1)
        c = jnp.einsum('bqk,bkd->bqd', e, key)
        return c

    def _L0_ffn_ref(x, qweight, weight_scale, weight_zero_point, bias):
        import jax, jax.numpy as jnp
        import numpy as np
        IN_FEATURES = 2048

        def _dequantize(qweight, scale, zero_point):
            N, K_packed = qweight.shape
            groups = K_packed // 3
            p = qweight.reshape(N, groups, 3)
            v0 = p[:, :, 0] & 63
            v1 = p[:, :, 0] >> 6 & 63
            v2 = p[:, :, 1] & 63
            v3 = p[:, :, 2] & 63
            unpacked = jnp.stack([v0, v1, v2, v3], axis=2).reshape(N, groups * 4)
            unpacked = unpacked[:, :IN_FEATURES]
            return (unpacked.astype(jnp.float32) - zero_point) * scale
        w = _dequantize(qweight, weight_scale, weight_zero_point)
        return jnp.einsum('bsk,nk->bsn', x, w) + bias
    x = x + jnp.tanh(g_xattn[0]) * _L0_xattn_ref(_layernorm(x, axis=-1), ctx_4096)
    x = x + jnp.tanh(g_ffn[0]) * _L0_ffn_ref(_layernorm(x, axis=-1), L0_ffn_qweight, L0_ffn_weight_scale, L0_ffn_weight_zero_point, L0_ffn_bias)
    return x

_drawn_inputs = setup_inputs


def setup_inputs(seed=0):
    import zlib

    import numpy as np

    out = dict(_drawn_inputs(seed))
    spreads = {}
    factors = {}
    for name, (base, spread) in spreads.items():
        noise = np.random.default_rng([zlib.crc32(name.encode()), seed]).standard_normal(out[name].shape)
        drawn = base * np.exp(spread * noise) if base else spread * noise
        out[name] = jnp.asarray(drawn.astype(out[name].dtype))
    for name, factor in factors.items():
        out[name] = (out[name] * factor).astype(out[name].dtype)
    return out
```

```python
from contextlib import ExitStack

import concourse.bass as bass
from concourse import mybir

F32 = mybir.dt.float32
F16 = mybir.dt.float16
BF16 = mybir.dt.bfloat16
I32 = mybir.dt.int32
U16 = mybir.dt.uint16
ALU = mybir.AluOpType
ACT = mybir.ActivationFunctionType
AX = mybir.AxisListType

HI, LO = 1, 0
EPS = 1e-5
X_SCALE = 256.0
P_SCALE = 4096.0
C_TOP = 2.0 ** 14
BIAS16 = 1024 + 32
TINY = 2.0 ** -100


def flamingo_block(nc, x, ctx_in, g_xattn, g_ffn, qweight, wscale, wzero, wbias, out):
    B, R, D = x.shape
    K = ctx_in.shape[1]
    N, WP = qweight.shape
    P = 128
    CH = D // P
    GW = K // 2
    assert K % 2 == 0 and GW <= 512 and R <= P
    ROWS = [P, P, GW - 2 * P] * 2
    FIRST = [0, P, 2 * P, GW, GW + P, GW + 2 * P]
    NT = len(ROWS)
    NCH = D // 512
    NB = N // P
    G4 = D // 4
    HB = B // 2
    HR = HB * R
    RING = 8
    QPB = P // 32

    with ExitStack() as stack:
        def sb(name, shape, dt=F32):
            return stack.enter_context(nc.sbuf_tensor(name, shape, dt))

        def psum(name):
            return stack.enter_context(nc.psum_tensor(name, [P, 512], F32))

        def sem(name):
            return stack.enter_context(nc.semaphore(name))

        x1_dram = nc.dram_tensor("x1_scratch", (B, R, D), F32, kind="Internal").ap()
        xT_dram = nc.dram_tensor("xT_scratch", (B, P, CH * R), F32, kind="Internal").ap()

        arena = sb("arena", [P, 2 * NT * D + 2 * D + NT * D + RING * GW])
        at = [0]

        def cut(words):
            at[0] += words
            return arena[:, at[0] - words:at[0]]

        pair = cut(2 * NT * D).bitcast(F16).rearrange("p (s d h) -> p s d h", s=2 * NT, h=2)
        xa = cut(D)
        xres = cut(D)
        raw = cut(NT * D).rearrange("p (t d) -> p t d", t=NT)
        ring = cut(RING * GW).rearrange("p (s k) -> p s k", s=RING)
        pair_words = arena[:, 0:2 * NT * D].rearrange("p (s d) -> p s d", s=2 * NT)
        at[0] = 0
        wraw = cut(2 * WP).bitcast(I32).rearrange("p (s w) -> p s w", s=2)
        unp = cut(D).bitcast(U16).rearrange("p (s j g) -> p s j g", s=2, j=4)
        wT = cut(D).bitcast(F16).rearrange("p (s c n) -> p s c n", s=2, c=CH)
        yT = cut(2 * HR).rearrange("p (h r) -> p h r", h=2)
        cB = cut(N)
        assert at[0] <= NT * D
        at[0] = NT * D
        x1f = cut(B * D).rearrange("p (b d) -> p b d", b=B)
        xT = cut(B * CH * R)
        xT_words = xT.rearrange("p (b w) -> p b w", b=B)
        xTv = xT.bitcast(F16).rearrange("p (b c r h) -> p b c r h", b=B, c=CH, h=2)
        scB = cut(N)
        assert at[0] <= 3 * NT * D + 2 * D + RING * GW

        rows = sb("rows", [P, D])
        rows16 = rows[:].bitcast(F16).rearrange("p (d h) -> p d h", h=2)
        qT = sb("qT", [P, 2, CH * R])
        qT16 = qT[:].bitcast(F16).rearrange("p s (c r h) -> p s c r h", c=CH, h=2)
        junk = qT[:, :, 0:D // 2].bitcast(BF16)
        xTst = sb("xTst", [P, CH * R])
        E = sb("E", [P, 2, GW])
        prob = sb("prob", [P, K])
        prob16 = prob[:].bitcast(F16).rearrange("p (k h) -> p k h", h=2)
        pT = sb("pT", [P, NT, R])
        pT16 = pT[:].bitcast(F16).rearrange("p t (r h) -> p t r h", h=2)
        ring16 = ring.bitcast(F16).rearrange("p s (k h) -> p s k h", h=2)
        ident = sb("ident", [P, P])
        ident16 = sb("ident16", [P, P], F16)
        am = sb("am", [P, NT])
        sc = sb("sc", [P, 4])
        sc2 = sb("sc2", [P, 2, 4])
        soft = sb("soft", [P, 6])
        stats = sb("stats", [P, NCH, 6])
        mr = sb("mr", [P, 3])
        ln = sb("ln", [P, 6])
        half = sb("half", [P, 1])
        mrall = sb("mrall", [P, B, 2])
        negm = sb("negm", [P, B])
        rsum = sb("rsum", [P, B])
        rs8 = sb("rs8", [P, B])
        gates = sb("gates", [P, 2])
        tg = sb("tg", [P, 3])
        sn = sb("sn", [P, NB])
        bn = sb("bn", [P, NB])

        turn = [psum(f"turn{k}") for k in range(4)]
        S = stack.enter_context(nc.psum_tensor("S", [P, 2, 2, 512], F32))
        PV = turn[2:4]
        Y = [S[:, 0, h, :] for h in range(2)]

        s_raw = [sem(f"s_raw{t}") for t in range(NT)]
        s_xa = sem("s_xa")
        s_xres = sem("s_xres")
        s_const = sem("s_const")
        s_x1out = sem("s_x1out")
        s_xTfree = sem("s_xTfree")
        s_x1in = sem("s_x1in")
        s_xTin = sem("s_xTin")
        s_bc = sem("s_bc")
        s_w = [sem(f"s_w{k}") for k in range(2)]
        s_out = sem("s_out")
        s_id0 = sem("s_id0")
        s_id = sem("s_id")
        s_am0 = sem("s_am0")
        s_am = sem("s_am")
        s_amp = sem("s_amp")
        s_amall = sem("s_amall")
        s_clamp = sem("s_clamp")
        s_pow2 = sem("s_pow2")
        s_inv = sem("s_inv")
        s_scale = sem("s_scale")
        s_hi = sem("s_hi")
        s_lo = sem("s_lo")
        s_turned = [sem(f"s_turned{k}") for k in range(4)]
        s_evac = [sem(f"s_evac{k}") for k in range(4)]
        s_scores = sem("s_scores")
        s_nmax = sem("s_nmax")
        s_kneg = sem("s_kneg")
        s_exp = sem("s_exp")
        s_phi = sem("s_phi")
        s_plo = sem("s_plo")
        s_rcp = sem("s_rcp")
        s_coef = sem("s_coef")
        s_pvn = sem("s_pvn")
        s_x1 = sem("s_x1")
        s_stat = sem("s_stat")
        s_aggr = sem("s_aggr")
        s_var = sem("s_var")
        s_pow = sem("s_pow")
        s_nt = sem("s_nt")
        s_rstd = sem("s_rstd")
        s_keep = sem("s_keep")
        s_xn = sem("s_xn")
        s_xhi = sem("s_xhi")
        s_qrows = sem("s_qrows")
        s_frows = sem("s_frows")
        s_half = sem("s_half")
        s_tanh = sem("s_tanh")
        s_tgq = sem("s_tgq")
        s_coefs = sem("s_coefs")
        s_negm = sem("s_negm")
        s_rsA = sem("s_rsA")
        s_rsD = sem("s_rsD")
        s_rs8 = sem("s_rs8")
        s_u1 = sem("s_u1")
        s_u = sem("s_u")
        s_y = sem("s_y")
        s_yev = sem("s_yev")
        s_yb = sem("s_yb")
        s_zp = sem("s_zp")
        s_held = sem("s_held")
        s_cB = sem("s_cB")
        s_r1 = sem("s_r1")
        s_add = sem("s_add")

        HALF = CH // 2
        QU = CH // QPB // 2
        GU = CH // 4
        PRO = (2 * QU + 3 * GU + 1, 3 * GU)
        STEP = (2 * QU + 2 * GU + 1, 2 * GU)
        LAST = B - 1

        class Uses:

            def __init__(self, turn_first, pv_first):
                self.first, self.n = (turn_first, pv_first), [0, 0]

            def take(self, k):
                self.n[0] += k
                return self.first[0] + (self.n[0] - k)

            def group(self):
                at = [f + n for f, n in zip(self.first, self.n)]
                self.n = [n + GU for n in self.n]
                return at

        def chunk_use(group, c):
            return c % 4, group[c % 4 // 2] + c // 4

        def step_uses(i):
            return Uses(i * STEP[0] + PRO[0], i * STEP[1] + PRO[1])

        W_USE = PRO[0] + (B - 1) * STEP[0] - QU - GU
        C_LAST = W_USE + 1

        def w_use(n):
            return n + (C_LAST + QU - 1) if not isinstance(n, int) or n > 0 else W_USE

        def ln_first(i):
            return i * 2 + 2

        HI_AT = (2, 6, 10)
        HI2_AT = (3, 7, 11)
        ROWS_AT = 13
        PROBS_AT, PHI_AT = 2, 4
        DVE_CHUNKS = (5, 9, 12, 14)
        PLO_AT = 5
        LO2_AT = (4, 8, 11)

        LN2_6, LN2_7 = 2 * B - 2, 2 * B - 1

        def unrolled(eng, step):
            with eng.Fori(0, (B - 2) // 2) as j:
                step(j * 2, 0, True)
                step(j * 2 + 1, 1, True)
            step(B - 2, 0, False)

        def w_steps(eng, step):
            step(0, 0, 0)
            with eng.Fori(0, (NB - 4) // 2) as j:
                step(j * 2 + 1, 1, j)
                step(j * 2 + 2, 0, j + 1)
            for n in range(NB - 3, NB):
                step(n, n % 2, n // 2)

        def hold(eng, s, value):
            eng.wait_ge(s, value)
            if not isinstance(value, int):
                eng.sem_inc(s_held, 1)

        block = stack.enter_context(nc.Block())

        @block.sync
        def _(sp):
            def load_ctx(b, t):
                sp.dma_start(raw[0:ROWS[t], t, :], ctx_in[b, FIRST[t]:FIRST[t] + ROWS[t], :]).then_inc(s_raw[t], 16)

            sp.dma_start(xa[0:R, :], x[0]).then_inc(s_xa, 16)
            for t in range(NT):
                load_ctx(0, t)
            sp.dma_start(gates[:, 0:1], g_xattn.partition_broadcast(P)).then_inc(s_const, 16)
            sp.dma_start(gates[:, 1:2], g_ffn.partition_broadcast(P)).then_inc(s_const, 16)
            sp.wait_ge(s_qrows, 1)
            sp.dma_start(xa[0:R, :], x[1]).then_inc(s_xa, 16)
            for t in range(NT):
                sp.wait_ge(s_lo, t + 1)
                load_ctx(1, t)
            sp.dma_start(sn[:, :], wscale.rearrange("(t p) o -> p (t o)", p=P), allow_slow_non_contiguous=True).then_inc(s_const, 16)
            sp.dma_start(bn[:, :], wbias.rearrange("(t p) -> p t", p=P), allow_slow_non_contiguous=True).then_inc(s_const, 16)

            with sp.Fori(2, B) as b:
                sp.wait_ge(s_qrows, b)
                sp.dma_start(xa[0:R, :], x[b]).then_inc(s_xa, 16)
                for t in range(NT):
                    sp.wait_ge(s_lo, b * NT + (t + 1 - NT))
                    load_ctx(b, t)
            sp.wait_ge(s_pvn, NCH * (B - 1))
            for n in range(2):
                sp.dma_start(wraw[:, n, :], qweight[n * P:(n + 1) * P, :]).then_inc(s_w[n], 16)
            sp.dma_start(cB[0:R, :], wzero.rearrange("n o -> (n o)").partition_broadcast(R)).then_inc(s_bc, 16)
            sp.wait_ge(s_scores, 2 * B)
            sp.dma_start(scB[0:R, :], wscale.rearrange("n o -> (n o)").partition_broadcast(R)).then_inc(s_bc, 16)
            sp.wait_ge(s_xTfree, 16 * B)
            for b in range(B - 1):
                sp.dma_start(xT_words[:, b, :], xT_dram[b]).then_inc(s_xTin, 16)
            sp.wait_ge(s_x1out, 16 * B)
            sp.wait_ge(s_frows, B)
            sp.wait_ge(s_pvn, NCH * B)
            for b in range(B):
                sp.dma_start(x1f[0:R, b, :], x1_dram[b]).then_inc(s_x1in, 16)

            def w_step(n, par, k):
                if not isinstance(n, int) or n + 2 < NB:
                    sp.wait_ge(s_u, n + 1)
                    sp.dma_start(wraw[:, par, :], qweight[bass.ds((n + 2) * P, P), :]).then_inc(s_w[par], 16)
                if not (isinstance(n, int) and n == 0):
                    sp.wait_ge(s_add, n * 2)
                    store(n - 1)

            def store(n):
                sp.dma_start(out.rearrange("b r n -> r b n")[:, :, bass.ds(n * P, P)],
                             x1f[0:R, :, bass.ds(n * P, P)]).then_inc(s_out, 16)

            w_steps(sp, w_step)
            sp.wait_ge(s_add, 2 * NB)
            store(NB - 1)
            sp.wait_ge(s_out, 16 * NB)

        @block.gpsimd
        def _(pool):
            pool.memset(ident[:, :], 0.0).then_inc(s_id0, 1)
            pool.memset(ident16[:, :], 0.0).then_inc(s_id0, 1)
            pool.memset(half[:, :], -0.5).then_inc(s_half, 1)
            pool.wait_ge(s_id0, 2)
            for m in (ident, ident16):
                pool.affine_select(out=m[:, :], in_=m[:, :], compare_op=ALU.not_equal, fill=1.0,
                                   base=0, pattern=[[-1, P]], channel_multiplier=1).then_inc(s_id, 1)
            pool.wait_ge(s_half, 1)

            def rstd(q):
                vt, y0, a, c, nm = (ln[0:R, k:k + 1] for k in range(5))
                hold(pool, s_aggr, q + 1)
                pool.tensor_scalar(nm, mr[0:R, 0:1], -1.0, None, ALU.mult)
                pool.tensor_scalar(vt, mr[0:R, 1:2], EPS, None, ALU.add).then_inc(s_var, 1)
                hold(pool, s_var, q + 1)
                pool.tensor_tensor(y0, vt, half[0:R, :], ALU.pow).then_inc(s_pow, 1)
                hold(pool, s_pow, q + 1)
                pool.tensor_tensor(a, y0, y0, ALU.mult).then_inc(s_nt, 1)
                hold(pool, s_nt, q * 3 + 1)
                pool.tensor_tensor(a, a, vt, ALU.mult).then_inc(s_nt, 1)
                hold(pool, s_nt, q * 3 + 2)
                pool.tensor_scalar(c, a, -0.5 * X_SCALE, 1.5 * X_SCALE, ALU.mult, ALU.add).then_inc(s_nt, 1)
                hold(pool, s_nt, q * 3 + 3)
                pool.tensor_tensor(mr[0:R, 1:2], y0, c, ALU.mult).then_inc(s_rstd, 1)
                hold(pool, s_rstd, q * 2 + 1)
                pool.tensor_tensor(mr[0:R, 2:3], mr[0:R, 1:2], nm, ALU.mult).then_inc(s_rstd, 1)

            def row_lo(q, src, rows_done):
                hold(pool, s_xhi, q + 1)
                pool.tensor_tensor(rows16[0:R, :, LO], src[0:R, :], rows16[0:R, :, HI], ALU.subtract).then_inc(rows_done, 1)

            def all_max(b):
                hold(pool, s_amp, b + 1)
                pool.partition_all_reduce(sc[:, 1:2], sc[:, 0:1], P, bass.bass_isa.ReduceOp.max).then_inc(s_amall, 1)

            def x1_out(i):
                hold(pool, s_x1, i * NCH + (NCH + 2))
                pool.dma_start(x1_dram[i], xres[0:R, :]).then_inc(s_x1out, 16)

            def x_in(i):
                hold(pool, s_frows, i)
                pool.dma_start(xres[0:R, :], x[i]).then_inc(s_xres, 16)

            pool.dma_start(xres[0:R, :], x[0]).then_inc(s_xres, 16)
            for b in range(2):
                rstd(b)
                row_lo(b, xa, s_qrows)
                all_max(b)
            with pool.Fori(0, B - 2) as i:
                rstd(i * 2 + 2)
                row_lo(i * 2 + 2, xa, s_qrows)
                all_max(i + 2)
                x1_out(i)
                rstd(i * 2 + 3)
                row_lo(i * 2 + 3, xres, s_frows)
                x_in(i + 1)
            x1_out(B - 2)
            rstd(LN2_6)
            row_lo(LN2_6, xres, s_frows)
            x_in(LAST)
            x1_out(LAST)
            rstd(LN2_7)
            row_lo(LN2_7, xres, s_frows)

        @block.scalar
        def _(act):
            def hi(b, par, t):
                n = ROWS[t]
                act.wait_ge(s_scale, b + 1)
                act.activation(pair[0:n, par * NT + t, :, HI], raw[0:n, t, :], ACT.Copy,
                               scale=sc2[0:n, par, 0:1]).then_inc(s_hi, 1)

            def row_norm(q):
                hold(act, s_rstd, q * 2 + 2)
                act.activation(xa[0:R, :], xa[0:R, :], ACT.Identity, scale=mr[0:R, 1:2], bias=mr[0:R, 2:3]).then_inc(s_xn, 1)

            def row_hi(q, src):
                act.wait_ge(s_xn, q + 1)
                act.activation(rows16[0:R, :, HI], src[0:R, :], ACT.Copy).then_inc(s_xhi, 1)

            def turned(k, u):
                act.wait_ge(s_turned[k], u + 1)

            def ring_out(g, c):
                k, u = chunk_use(g, c)
                turned(k, u)
                act.activation(ring[:, c % RING, :], turn[k][:, 0:GW], ACT.Copy).then_inc(s_evac[k], 1)

            def rows_out(u0, dst):
                for m in range(2 * QU):
                    turned(m % 2, u0 + m // 2)
                    c0 = m * QPB * R
                    act.activation(dst[:, c0:c0 + QPB * R], turn[m % 2][:, 0:QPB * R], ACT.Copy).then_inc(s_evac[m % 2], 1)

            def probs(i, par):
                act.wait_ge(s_kneg, i + 1)
                act.activation(E[0:R, :, :], S[0:R, par, :, 0:GW], ACT.Exp, bias=soft[0:R, 1:2],
                               scale=sc2[0:R, par, 1:2], accum_out=soft[0:R, 2:3]).then_inc(s_exp, 1)

            def prob_hi(i):
                act.wait_ge(s_exp, i + 1)
                act.activation(prob16[0:R, :, HI], E[0:R, :, :].rearrange("p g k -> p (g k)"), ACT.Copy,
                               scale=P_SCALE).then_inc(s_phi, 1)

            def pT_out(u):
                for k in range(2):
                    turned(k, u)
                    act.activation(pT[:, 3 * k:3 * k + 2, :], turn[k][:, 0:2 * R].rearrange("p (t r) -> p t r", r=R), ACT.Copy)
                    act.activation(pT[0:ROWS[2], 3 * k + 2, :], turn[k][0:ROWS[2], 2 * R:3 * R], ACT.Copy).then_inc(s_evac[k], 1)

            act.sem_inc(s_xTfree, 16)
            act.wait_ge(s_const, 64 - 32)
            act.activation(tg[:, 0:2], gates[:, :], ACT.Tanh).then_inc(s_tanh, 1)
            row_norm(0)
            row_hi(0, xa)
            u = Uses(0, 0)
            rows_out(u.take(QU), qT[:, 0, :])
            for t in range(3):
                hi(0, 0, t)
            g = u.group()
            for c in range(CH):
                ring_out(g, c)
                if c in (1, 4, 7):
                    hi(0, 0, 3 + c // 3)
            row_norm(1)
            row_hi(1, xa)
            g = u.group()
            for c in range(CH):
                ring_out(g, c)
                if c in (8, 10, 12):
                    hi(1, 1, (8, 10, 12).index(c))
            rows_out(u.take(QU), qT[:, 1, :])
            probs(0, 0)
            prob_hi(0)
            g = u.group()
            for c in range(CH):
                ring_out(g, c)
                if c in (1, 4, 7):
                    hi(1, 1, 3 + c // 3)
            pT_out(u.take(1))

            def step(i, par, full):
                u = step_uses(i)
                if full:
                    row_norm(ln_first(i))
                    row_hi(ln_first(i), xa)
                    rows_out(u.take(QU), qT[:, par, :])
                g = u.group()
                for c in range(CH):
                    ring_out(g, c)
                    if full and c in HI_AT:
                        t = HI_AT.index(c)
                        if t == 0:
                            act.wait_ge(s_pvn, i * NCH + NCH)
                        hi(i + 2, par, t)
                if full:
                    g = u.group()
                    for c in range(CH):
                        if c not in DVE_CHUNKS:
                            ring_out(g, c)
                        if c == PROBS_AT:
                            probs(i + 1, 1 - par)
                        if c == PHI_AT:
                            prob_hi(i + 1)
                        if c in HI2_AT:
                            hi(i + 2, par, 3 + HI2_AT.index(c))
                        if c == ROWS_AT:
                            row_hi(ln_first(i) + 1, xres)
                else:
                    probs(i + 1, 1 - par)
                    prob_hi(i + 1)
                    row_hi(LN2_6, xres)
                pT_out(u.take(1))
                act.wait_ge(s_xTfree, i * 16 + 16)
                c = u.take(QU)
                rows_out(c, xTst)
                for k in range(2):
                    hold(act, s_evac[k], c + QU)
                act.dma_start(xT_dram[i], xTst[:, :]).then_inc(s_xTfree, 16)

            unrolled(act, step)

            def w_out(n, par):
                turned(0, w_use(n))
                act.activation(wT[:, par, 0:HALF, :], turn[0][:, :].bitcast(F16).rearrange("p (c n) -> p c n", n=P),
                               ACT.Copy, bias=-float(BIAS16)).then_inc(s_evac[0], 1)

            w_out(0, 0)
            row_hi(LN2_7, xres)
            rows_out(C_LAST, xT_words[:, LAST, :])
            act.wait_ge(s_coefs, 1)

            def w_step(n, par, k):
                if not isinstance(n, int) or n + 1 < NB:
                    w_out(n + 1, 1 - par)
                for h in range(2):
                    hold(act, s_y, n * 2 + (h + 1))
                    act.activation(yT[:, h, :], Y[h][:, 0:HR], ACT.Identity, scale=sn[:, bass.ds(n, 1)],
                                   bias=bn[:, bass.ds(n, 1)]).then_inc(s_yev, 1)
                    if isinstance(n, int) and n == 0:
                        if h == 0:
                            act.wait_ge(s_x1in, 16 * B)
                            act.wait_ge(s_negm, 1)
                        for b in (range(0, 2), range(2, HB))[h]:
                            if b > 0:
                                act.wait_ge(s_rsA, b)
                            act.activation(junk[0:R, 0, :], x1f[0:R, b, :], ACT.Identity, bias=negm[0:R, b:b + 1],
                                           accum_out=rsum[0:R, b:b + 1]).then_inc(s_rsA, 1)

            w_steps(act, w_step)

        @block.vector
        def _(dve):
            def amax(b, t):
                dve.wait_ge(s_raw[t], b * 16 + 16)
                dve.tensor_reduce(am[0:ROWS[t], t:t + 1], raw[0:ROWS[t], t, :], AX.X, ALU.max,
                                  apply_absolute_value=True).then_inc(s_am, 1)

            def part_max(b):
                dve.wait_ge(s_am, b * NT + NT)
                dve.tensor_reduce(sc[:, 0:1], am[:, :], AX.X, ALU.max).then_inc(s_amp, 1)

            def scales(b, par):
                dve.wait_ge(s_amall, b + 1)
                dve.tensor_scalar(sc[:, 2:3], sc[:, 1:2], TINY, None, ALU.max).then_inc(s_clamp, 1)
                dve.wait_ge(s_clamp, b + 1)
                dve.tensor_scalar(sc[:, 3:4].bitcast(I32), sc[:, 2:3].bitcast(I32), 0x7F800000, None,
                                  ALU.bitwise_and).then_inc(s_pow2, 1)
                dve.wait_ge(s_pow2, b + 1)
                dve.reciprocal(sc2[:, par, 3:4], sc[:, 3:4]).then_inc(s_inv, 1)
                dve.tensor_scalar(sc2[:, par, 1:2], sc[:, 3:4], 1.0 / (C_TOP * X_SCALE), None, ALU.mult)
                dve.tensor_scalar(sc2[:, par, 2:3], sc[:, 3:4], 1.0 / (C_TOP * P_SCALE), None, ALU.mult)
                dve.wait_ge(s_inv, b + 1)
                dve.tensor_scalar(sc2[:, par, 0:1], sc2[:, par, 3:4], C_TOP, None, ALU.mult).then_inc(s_scale, 1)

            def lo(b, par, t):
                n = ROWS[t]
                dve.wait_ge(s_hi, b * NT + (t + 1))
                dve.scalar_tensor_tensor(out=pair[0:n, par * NT + t, :, LO], in0=raw[0:n, t, :],
                                         scalar=sc2[0:n, par, 0:1], in1=pair[0:n, par * NT + t, :, HI],
                                         op0=ALU.mult, op1=ALU.subtract).then_inc(s_lo, 1)

            def row_stats(q, src):
                for k in range(NCH):
                    dve.bn_stats(stats[0:R, k, :], src[0:R, k * 512:(k + 1) * 512]).then_inc(s_stat, 1)
                hold(dve, s_stat, q * NCH + NCH)
                if not (isinstance(q, int) and q == 0):
                    hold(dve, s_xn, q)
                dve.bn_aggr(mr[0:R, 0:2], stats[0:R, :, :].rearrange("p a b -> p (a b)")).then_inc(s_aggr, 1)

            def row_norm(i, q):
                dve.wait_ge(s_x1out, i * 16 + 16)
                dve.wait_ge(s_rstd, q * 2 + 2)
                dve.tensor_scalar(xres[0:R, :], xres[0:R, :], mr[0:R, 0:1], mr[0:R, 1:2], ALU.subtract,
                                  ALU.mult).then_inc(s_xn, 1)

            def keep(i):
                dve.tensor_copy(mrall[0:R, bass.ds(i, 1), :], mr[0:R, 0:2].rearrange("p (o c) -> p o c", o=1)).then_inc(s_keep, 1)

            def ring_out(g, c):
                k, u = chunk_use(g, c)
                dve.wait_ge(s_turned[k], u + 1)
                dve.tensor_copy(ring[:, c % RING, :], turn[k][:, 0:GW]).then_inc(s_evac[k], 1)

            def row_max(i, par):
                dve.wait_ge(s_scores, i * 2 + 2)
                dve.tensor_reduce(soft[0:R, 0:1], S[0:R, par, :, 0:GW], AX.XY, ALU.max, negate=True).then_inc(s_nmax, 1)
                dve.wait_ge(s_nmax, i + 1)
                dve.tensor_scalar(soft[0:R, 1:2], soft[0:R, 0:1], sc2[0:R, par, 1:2], None, ALU.mult).then_inc(s_kneg, 1)

            def prob_lo(i, par):
                dve.wait_ge(s_phi, i + 1)
                dve.scalar_tensor_tensor(out=prob16[0:R, :, LO], in0=E[0:R, :, :].rearrange("p g k -> p (g k)"), scalar=P_SCALE,
                                         in1=prob16[0:R, :, HI], op0=ALU.mult, op1=ALU.subtract).then_inc(s_plo, 1)
                dve.reciprocal(soft[0:R, 3:4], soft[0:R, 2:3]).then_inc(s_rcp, 1)
                dve.wait_ge(s_rcp, i + 1)
                dve.tensor_scalar(soft[0:R, 4:5], soft[0:R, 3:4], sc2[0:R, par, 2:3], tg[0:R, 0:1], ALU.mult,
                                  ALU.mult).then_inc(s_coef, 1)

            def x1_piece(i, n):
                if n == 0:
                    dve.wait_ge(s_coef, i + 1)
                    dve.wait_ge(s_xres, i * 16 + 16)
                dve.wait_ge(s_pvn, i * NCH + (n + 1))
                piece = xres[0:R, n * 512:(n + 1) * 512]
                dve.scalar_tensor_tensor(out=piece, in0=PV[n % 2][0:R, :], scalar=soft[0:R, 4:5], in1=piece,
                                         op0=ALU.mult, op1=ALU.add).then_inc(s_x1, 1)

            dve.memset(am[:, :], 0.0).then_inc(s_am0, 1)
            dve.sem_inc(s_x1, 2)
            dve.wait_ge(s_xa, 16)
            row_stats(0, xa)
            dve.wait_ge(s_am0, 1)
            for t in range(NT):
                amax(0, t)
            part_max(0)
            scales(0, 0)
            for t in range(NT):
                lo(0, 0, t)
            dve.wait_ge(s_xa, 32)
            row_stats(1, xa)
            for t in range(NT):
                amax(1, t)
            part_max(1)
            scales(1, 1)
            for t in range(3):
                lo(1, 1, t)
            dve.wait_ge(s_tanh, 1)
            row_max(0, 0)
            prob_lo(0, 0)
            for t in range(3, NT):
                lo(1, 1, t)
            dve.tensor_scalar(tg[:, 2:3], tg[:, 1:2], 1.0 / X_SCALE, None, ALU.mult).then_inc(s_tgq, 1)
            dve.wait_ge(s_const, 64)
            dve.wait_ge(s_tgq, 1)
            dve.tensor_scalar(sn[:, :], sn[:, :], tg[:, 2:3], None, ALU.mult)
            dve.tensor_scalar(bn[:, :], bn[:, :], tg[:, 1:2], None, ALU.mult).then_inc(s_coefs, 1)

            def step(i, par, full):
                if full:
                    dve.wait_ge(s_xa, i * 16 + 48)
                    row_stats(ln_first(i), xa)
                    amax(i + 2, 0)
                x1_piece(i, 0)
                if full:
                    amax(i + 2, 1)
                x1_piece(i, 1)
                if full:
                    amax(i + 2, 2)
                    amax(i + 2, 3)
                x1_piece(i, 2)
                if full:
                    amax(i + 2, 4)
                    amax(i + 2, 5)
                    part_max(i + 2)
                x1_piece(i, 3)
                if full:
                    scales(i + 2, par)
                q = ln_first(i) + 1 if full else LN2_6
                dve.wait_ge(s_x1, i * NCH + (NCH + 2))
                if full:
                    lo(i + 2, par, 0)
                row_stats(q, xres)
                if full:
                    lo(i + 2, par, 1)
                row_norm(i, q)
                keep(i)
                if full:
                    lo(i + 2, par, 2)
                row_max(i + 1, 1 - par)
                if full:
                    u = step_uses(i)
                    u.take(QU)
                    u.group()
                    g = u.group()
                    for c in range(CH):
                        if c in DVE_CHUNKS:
                            ring_out(g, c)
                        if c == PLO_AT:
                            prob_lo(i + 1, 1 - par)
                        if c in LO2_AT:
                            lo(i + 2, par, 3 + LO2_AT.index(c))
                else:
                    prob_lo(i + 1, 1 - par)

            unrolled(dve, step)

            def unpack(n, par, k):
                dve.wait_ge(s_w[par], k * 16 + 16)
                p = wraw[:, par, :].bitcast(U16).rearrange("p (g w h) -> p g w h", w=3, h=2)
                dve.tensor_scalar(unp[:, par, 1, :], p[:, :, 0, 0], 6, 63, ALU.logical_shift_right,
                                  ALU.bitwise_and).then_inc(s_u1, 1)
                for j, w in ((0, 0), (2, 1), (3, 2)):
                    dve.tensor_scalar(unp[:, par, j, :], p[:, :, w, 0], 63, 0x6400, ALU.bitwise_and, ALU.bitwise_or)
                dve.wait_ge(s_u1, n + 1)
                dve.tensor_scalar(unp[:, par, 1, :], unp[:, par, 1, :], 0x6400, None, ALU.bitwise_or).then_inc(s_u, 1)

            def w_out(n, par):
                dve.wait_ge(s_turned[1], w_use(n) + 1)
                dve.tensor_scalar(wT[:, par, HALF:CH, :], turn[1][:, :].bitcast(F16).rearrange("p (c n) -> p c n", n=P),
                                  -float(BIAS16), None, ALU.add).then_inc(s_evac[1], 1)

            unpack(0, 0, 0)
            x1_piece(LAST, 0)
            x1_piece(LAST, 1)
            unpack(1, 1, 0)
            x1_piece(LAST, 2)
            x1_piece(LAST, 3)
            dve.wait_ge(s_x1, NCH * B + 2)
            row_stats(LN2_7, xres)
            w_out(0, 0)
            row_norm(LAST, LN2_7)
            keep(LAST)
            dve.wait_ge(s_keep, B)
            dve.tensor_scalar(negm[0:R, :], mrall[0:R, :, 0], -1.0, None, ALU.mult).then_inc(s_negm, 1)
            dve.wait_ge(s_bc, 32)
            dve.tensor_scalar(cB[0:R, :], cB[0:R, :], -1.0, 32.0, ALU.mult, ALU.add).then_inc(s_zp, 1)
            dve.wait_ge(s_zp, 1)
            dve.scalar_tensor_tensor(out=cB[0:R, :], in0=cB[0:R, :], scalar=tg[0:R, 2:3], in1=scB[0:R, :],
                                     op0=ALU.mult, op1=ALU.mult).then_inc(s_cB, 1)

            def row_sums():
                dve.wait_ge(s_x1in, 16 * B)
                for b in range(HB, B):
                    if b > HB:
                        dve.wait_ge(s_rsD, b - HB)
                    dve.tensor_scalar(junk[0:R, 1, :], x1f[0:R, b, :], mrall[0:R, b, 0:1], 0.0, ALU.subtract, ALU.add,
                                      accum_out=rsum[0:R, b:b + 1]).then_inc(s_rsD, 1)
                dve.wait_ge(s_rsD, HB)
                dve.wait_ge(s_rsA, HB)
                dve.tensor_tensor(rs8[0:R, :], rsum[0:R, :], mrall[0:R, :, 1], ALU.mult).then_inc(s_rs8, 1)
                dve.wait_ge(s_rs8, 1)
                dve.wait_ge(s_cB, 1)

            def rank_one(n):
                cols = bass.ds(n * P, P)
                for b in range(B):
                    last = dve.scalar_tensor_tensor(out=x1f[0:R, b, cols], in0=cB[0:R, cols], scalar=rs8[0:R, b:b + 1],
                                                    in1=x1f[0:R, b, cols], op0=ALU.mult, op1=ALU.add)
                last.then_inc(s_r1, 1)

            def add_up(n, h):
                dve.wait_ge(s_yb, n * 2 + (h + 1))
                block_of = x1f[0:R, h * HB:(h + 1) * HB, bass.ds(n * P, P)]
                dve.tensor_tensor(block_of, PV[h][0:R, :].rearrange("p (b n) -> p b n", b=HB), block_of,
                                  ALU.add).then_inc(s_add, 1)

            def w_step(n, par, k):
                first = isinstance(n, int) and n == 0
                if not isinstance(n, int) or n + 1 < NB:
                    w_out(n + 1, 1 - par)
                if not isinstance(n, int) or n + 2 < NB:
                    unpack(n + 2, par, k + 1)
                if first:
                    row_sums()
                if not first:
                    add_up(n - 1, 1)
                rank_one(n)
                dve.wait_ge(s_r1, n + 1)
                add_up(n, 0)

            w_steps(dve, w_step)
            add_up(NB - 1, 1)

        @block.tensor
        def _(pe):
            def free(k, u):
                if not (isinstance(u, int) and u == 0):
                    pe.wait_ge(s_evac[k], u)

            def turn_rows(u0, ready, b, columns):
                pe.wait_ge(ready, b + 1)
                for m in range(2 * QU):
                    free(m % 2, u0 + m // 2)
                    for k in range(QPB):
                        last = pe.transpose(turn[m % 2][:, k * R:(k + 1) * R], columns(m * QPB + k), ident[0:R, 0:R])
                    last.then_inc(s_turned[m % 2], 1)

            def q_cols(c):
                return rows[0:R, c * P:(c + 1) * P]

            def ffn_cols(c):
                j, gb = divmod(c, G4 // P)
                return rows[0:R, 4 * gb * P + j:4 * (gb + 1) * P:4]

            def score_group(b, par, g, u0, attended=lambda: None):
                pe.wait_ge(s_lo, b * NT + (3 * g + 3))
                for c in range(CH + 4):
                    if c < CH:
                        bank, use = chunk_use(u0, c)
                        free(bank, use)
                        if c == 2:
                            attended()
                        for t in range(3):
                            n = ROWS[3 * g + t]
                            last = pe.transpose(turn[bank][:, t * P:t * P + n],
                                                pair_words[0:n, par * NT + 3 * g + t, c * P:(c + 1) * P],
                                                ident[0:n, 0:n])
                        last.then_inc(s_turned[bank], 1)
                    if c >= 4:
                        m = c - 4
                        bank, use = chunk_use(u0, m)
                        pe.wait_ge(s_evac[bank], use + 1)
                        for k, (a, e) in enumerate(((HI, HI), (HI, LO), (LO, HI))):
                            last = pe.matmul(S[0:R, par, g, 0:GW], qT16[:, par, m, :, a], ring16[:, m % RING, :, e],
                                             start=(m == 0 and k == 0), stop=(m == CH - 1 and k == 2))
                last.then_inc(s_scores, 1)

            def turn_probs(i, u):
                pe.wait_ge(s_plo, i + 1)
                for t in range(NT):
                    k = t // 3
                    if t % 3 == 0:
                        free(k, u)
                    n = ROWS[t]
                    last = pe.transpose(turn[k][0:n, (t % 3) * R:(t % 3 + 1) * R], prob[0:R, FIRST[t]:FIRST[t] + n],
                                        ident[0:R, 0:R])
                    if t % 3 == 2:
                        last.then_inc(s_turned[k], 1)

            def probs_turned(u):
                for k in range(2):
                    pe.wait_ge(s_evac[k], u + 1)

            def attend(i, par):
                for n in range(NCH):
                    pe.wait_ge(s_x1, i * NCH + (n + 1))
                    for t in range(NT):
                        r = ROWS[t]
                        for k, (a, e) in enumerate(((HI, HI), (HI, LO), (LO, HI))):
                            last = pe.matmul(PV[n % 2][0:R, :], pT16[0:r, t, :, a],
                                             pair[0:r, par * NT + t, n * 512:(n + 1) * 512, e],
                                             start=(t == 0 and k == 0), stop=(t == NT - 1 and k == 2))
                    last.then_inc(s_pvn, 1)

            pe.wait_ge(s_id, 2)
            u = Uses(0, 0)
            turn_rows(u.take(QU), s_qrows, 0, q_cols)
            score_group(0, 0, 0, u.group())
            score_group(0, 0, 1, u.group())
            turn_rows(u.take(QU), s_qrows, 1, q_cols)
            score_group(1, 1, 0, u.group())
            probs = u.take(1)
            turn_probs(0, probs)
            probs_turned(probs)

            def step(i, par, full):
                u = step_uses(i)
                attend(i, par)
                if full:
                    turn_rows(u.take(QU), s_qrows, i + 2, q_cols)
                score_group(i + 1, 1 - par, 1, u.group(),
                            attended=lambda: pe.wait_ge(s_x1, i * NCH + (NCH + 2)))
                if full:
                    score_group(i + 2, par, 0, u.group())
                probs = u.take(1)
                turn_probs(i + 1, probs)
                turn_rows(u.take(QU), s_frows, i, ffn_cols)
                probs_turned(probs)

            unrolled(pe, step)

            def turn_weights(n, par):
                pe.wait_ge(s_u, n + 1)
                for c in range(CH):
                    if c % HALF == 0:
                        free(c // HALF, w_use(n))
                    j, gb = divmod(c, G4 // P)
                    last = pe.transpose(turn[c // HALF][:, :].bitcast(F16)[:, (c % HALF) * P:(c % HALF + 1) * P],
                                        unp[:, par, j, gb * P:(gb + 1) * P].bitcast(F16), ident16[:, :])
                    if c % HALF == HALF - 1:
                        last.then_inc(s_turned[c // HALF], 1)

            def multiply(n, par, h):
                if not (isinstance(n, int) and n == 0):
                    pe.wait_ge(s_yev, n * 2 + (h - 1))
                for c in range(CH):
                    for k in (HI, LO):
                        last = pe.matmul(Y[h][:, 0:HR], wT[:, par, c, :], xTv[:, h * HB:(h + 1) * HB, c, :, k],
                                         start=(c == 0 and k == HI), stop=(c == CH - 1 and k == LO))
                last.then_inc(s_y, 1)

            def turn_back(n, h):
                pe.wait_ge(s_yev, n * 2 + (h + 1))
                if not (isinstance(n, int) and n == 0):
                    pe.wait_ge(s_add, n * 2 + (h - 1))
                for b in range(HB):
                    last = pe.transpose(PV[h][0:R, b * P:(b + 1) * P], yT[:, h, b * R:(b + 1) * R], ident[:, :])
                last.then_inc(s_yb, 1)

            attend(LAST, 1)
            turn_weights(0, 0)
            turn_rows(C_LAST, s_frows, LAST, ffn_cols)
            pe.wait_ge(s_xTin, 16 * (B - 1))
            pe.wait_ge(s_x1, NCH * B + 2)

            def w_step(n, par, k):
                for q in range(2):
                    pe.wait_ge(s_evac[q], w_use(n) + 1 if not (isinstance(n, int) and n == 0) else C_LAST + QU)
                if not isinstance(n, int) or n + 1 < NB:
                    turn_weights(n + 1, 1 - par)
                multiply(n, par, 0)
                if not (isinstance(n, int) and n == 0):
                    turn_back(n - 1, 1)
                multiply(n, par, 1)
                turn_back(n, 0)

            w_steps(pe, w_step)
            turn_back(NB - 1, 1)


_INS = ["x", "ctx_4096", "g_xattn", "g_ffn", "L0_ffn_qweight", "L0_ffn_weight_scale", "L0_ffn_weight_zero_point", "L0_ffn_bias"]


def kernel(**inputs):
    import numpy as np
    import concourse.bacc as bacc
    from concourse.bass_utils import run_bass_kernel_spmd

    nc = bacc.Bacc("TRN2", target_bir_lowering=False, num_devices=1)
    arrays, args = {}, []
    for name in _INS:
        a = np.ascontiguousarray(inputs[name])
        arrays[f"in_{name}"] = a
        args.append(nc.dram_tensor(f"in_{name}", a.shape, mybir.dt.from_np(a.dtype), kind="ExternalInput").ap())
    shape = np.asarray(inputs["x"]).shape
    args.append(nc.dram_tensor("out_y", shape, F32, kind="ExternalOutput").ap())
    flamingo_block(nc, *args)
    r = run_bass_kernel_spmd(nc, [arrays], core_ids=[0])
    return r.results[0]["out_y"]
```

```python
from contextlib import ExitStack

import concourse.bass as bass
from concourse import mybir

F32 = mybir.dt.float32
F16 = mybir.dt.float16
BF16 = mybir.dt.bfloat16
I32 = mybir.dt.int32
U16 = mybir.dt.uint16
ALU = mybir.AluOpType
ACT = mybir.ActivationFunctionType
AX = mybir.AxisListType

HI, LO = 1, 0
EPS = 1e-5
X_SCALE = 256.0
P_SCALE = 4096.0
C_TOP = 2.0 ** 14
BIAS16 = 1024 + 32
TINY = 2.0 ** -100


def flamingo_block(nc, x, ctx_in, g_xattn, g_ffn, qweight, wscale, wzero, wbias, out):
    B, R, D = x.shape
    K = ctx_in.shape[1]
    N, WP = qweight.shape
    P = 128
    CH = D // P
    GW = K // 2
    assert K % 2 == 0 and GW <= 512 and R <= P
    ROWS = [P, P, GW - 2 * P] * 2
    FIRST = [0, P, 2 * P, GW, GW + P, GW + 2 * P]
    NT = len(ROWS)
    NCH = D // 512
    NB = N // P
    G4 = D // 4
    HB = B // 2
    HR = HB * R
    RING = 8
    QPB = P // 32

    with ExitStack() as stack:
        def sb(name, shape, dt=F32):
            return stack.enter_context(nc.sbuf_tensor(name, shape, dt))

        def psum(name):
            return stack.enter_context(nc.psum_tensor(name, [P, 512], F32))

        def sem(name):
            return stack.enter_context(nc.semaphore(name))

        x1_dram = nc.dram_tensor("x1_scratch", (B, R, D), F32, kind="Internal").ap()
        xT_dram = nc.dram_tensor("xT_scratch", (B, P, CH * R), F32, kind="Internal").ap()

        arena = sb("arena", [P, 2 * NT * D + 2 * D + NT * D + RING * GW])
        at = [0]

        def cut(words):
            at[0] += words
            return arena[:, at[0] - words:at[0]]

        pair = cut(2 * NT * D).bitcast(F16).rearrange("p (s d h) -> p s d h", s=2 * NT, h=2)
        xa = cut(D)
        xres = cut(D)
        raw = cut(NT * D).rearrange("p (t d) -> p t d", t=NT)
        ring = cut(RING * GW).rearrange("p (s k) -> p s k", s=RING)
        pair_words = arena[:, 0:2 * NT * D].rearrange("p (s d) -> p s d", s=2 * NT)
        at[0] = 0
        wraw = cut(2 * WP).bitcast(I32).rearrange("p (s w) -> p s w", s=2)
        unp = cut(D).bitcast(U16).rearrange("p (s j g) -> p s j g", s=2, j=4)
        wT = cut(D).bitcast(F16).rearrange("p (s c n) -> p s c n", s=2, c=CH)
        yT = cut(2 * HR).rearrange("p (h r) -> p h r", h=2)
        cB = cut(N)
        assert at[0] <= NT * D
        at[0] = NT * D
        x1f = cut(B * D).rearrange("p (b d) -> p b d", b=B)
        xT = cut(B * CH * R)
        xT_words = xT.rearrange("p (b w) -> p b w", b=B)
        xTv = xT.bitcast(F16).rearrange("p (b c r h) -> p b c r h", b=B, c=CH, h=2)
        scB = cut(N)
        assert at[0] <= 3 * NT * D + 2 * D + RING * GW

        rows = sb("rows", [P, D])
        rows16 = rows[:].bitcast(F16).rearrange("p (d h) -> p d h", h=2)
        qT = sb("qT", [P, 2, CH * R])
        qT16 = qT[:].bitcast(F16).rearrange("p s (c r h) -> p s c r h", c=CH, h=2)
        junk = qT[:, :, 0:D // 2].bitcast(BF16)
        xTst = sb("xTst", [P, CH * R])
        E = sb("E", [P, 2, GW])
        prob = sb("prob", [P, K])
        prob16 = prob[:].bitcast(F16).rearrange("p (k h) -> p k h", h=2)
        pT = sb("pT", [P, NT, R])
        pT16 = pT[:].bitcast(F16).rearrange("p t (r h) -> p t r h", h=2)
        ring16 = ring.bitcast(F16).rearrange("p s (k h) -> p s k h", h=2)
        ident = sb("ident", [P, P])
        ident16 = sb("ident16", [P, P], F16)
        am = sb("am", [P, NT])
        sc = sb("sc", [P, 4])
        sc2 = sb("sc2", [P, 2, 4])
        soft = sb("soft", [P, 6])
        stats = sb("stats", [P, NCH, 6])
        mr = sb("mr", [P, 2])
        ln = sb("ln", [P, 6])
        half = sb("half", [P, 1])
        mrall = sb("mrall", [P, B, 2])
        negm = sb("negm", [P, B])
        rsum = sb("rsum", [P, B])
        rs8 = sb("rs8", [P, B])
        gates = sb("gates", [P, 2])
        tg = sb("tg", [P, 3])
        sn = sb("sn", [P, NB])
        bn = sb("bn", [P, NB])

        turn = [psum(f"turn{k}") for k in range(4)]
        S = stack.enter_context(nc.psum_tensor("S", [P, 2, 2, 512], F32))
        BACK = turn[2:4]
        Y = [S[:, 0, h, :] for h in range(2)]

        s_raw = [sem(f"s_raw{t}") for t in range(NT)]
        s_xa = sem("s_xa")
        s_xres = sem("s_xres")
        s_const = sem("s_const")
        s_x1out = sem("s_x1out")
        s_xTfree = sem("s_xTfree")
        s_x1in = sem("s_x1in")
        s_xTin = sem("s_xTin")
        s_bc = sem("s_bc")
        s_w = [sem(f"s_w{k}") for k in range(2)]
        s_out = sem("s_out")
        s_id0 = sem("s_id0")
        s_id = sem("s_id")
        s_am0 = sem("s_am0")
        s_am = sem("s_am")
        s_amp = sem("s_amp")
        s_amall = sem("s_amall")
        s_clamp = sem("s_clamp")
        s_pow2 = sem("s_pow2")
        s_inv = sem("s_inv")
        s_scale = sem("s_scale")
        s_hi = sem("s_hi")
        s_lo = sem("s_lo")
        s_turned = [sem(f"s_turned{k}") for k in range(4)]
        s_evac = [sem(f"s_evac{k}") for k in range(4)]
        s_scores = sem("s_scores")
        s_nmax = sem("s_nmax")
        s_kneg = sem("s_kneg")
        s_exp = sem("s_exp")
        s_phi = sem("s_phi")
        s_plo = sem("s_plo")
        s_rcp = sem("s_rcp")
        s_coef = sem("s_coef")
        s_pvn = sem("s_pvn")
        s_pvt = sem("s_pvt")
        s_x1 = sem("s_x1")
        s_stat = sem("s_stat")
        s_aggr = sem("s_aggr")
        s_var = sem("s_var")
        s_pow = sem("s_pow")
        s_nt = sem("s_nt")
        s_rstd = sem("s_rstd")
        s_keep = sem("s_keep")
        s_xn = sem("s_xn")
        s_xhi = sem("s_xhi")
        s_qrows = sem("s_qrows")
        s_frows = sem("s_frows")
        s_half = sem("s_half")
        s_tanh = sem("s_tanh")
        s_tgq = sem("s_tgq")
        s_coefs = sem("s_coefs")
        s_negm = sem("s_negm")
        s_rsA = sem("s_rsA")
        s_rsD = sem("s_rsD")
        s_rs8 = sem("s_rs8")
        s_u1 = sem("s_u1")
        s_u = sem("s_u")
        s_y = sem("s_y")
        s_yev = sem("s_yev")
        s_yb = sem("s_yb")
        s_zp = sem("s_zp")
        s_held = sem("s_held")
        s_cB = sem("s_cB")
        s_r1 = sem("s_r1")
        s_add = sem("s_add")

        HALF = CH // 2
        QU = CH // QPB // 2
        GU = CH // 4
        PRO = (2 * QU + 3 * GU, 3 * GU + 1)
        STEP = (2 * QU + 2 * GU, 2 * GU + 1)
        LAST = B - 1

        class Uses:

            def __init__(self, low_first, high_first):
                self.first, self.n = (low_first, high_first), [0, 0]

            def take(self, k):
                self.n[0] += k
                return self.first[0] + (self.n[0] - k)

            def take_high(self, k):
                self.n[1] += k
                return self.first[1] + (self.n[1] - k)

            def group(self):
                at = [f + n for f, n in zip(self.first, self.n)]
                self.n = [n + GU for n in self.n]
                return at

        def chunk_use(group, c):
            return c % 4, group[c % 4 // 2] + c // 4

        def step_uses(i):
            return Uses(i * STEP[0] + PRO[0], i * STEP[1] + PRO[1])

        W_USE = PRO[0] + (B - 1) * STEP[0] - QU - GU
        C_LAST = W_USE + 1

        def w_use(n):
            return n + (C_LAST + QU - 1) if not isinstance(n, int) or n > 0 else W_USE

        def ln_first(i):
            return i * 2 + 2

        HI_AT, ROWS_AT = 3, 11
        PROBS_AT, PHI_AT = 2, 4

        LN2_6, LN2_7 = 2 * B - 2, 2 * B - 1

        def unrolled(eng, step):
            with eng.Fori(0, (B - 2) // 2) as j:
                step(j * 2, 0, True)
                step(j * 2 + 1, 1, True)
            step(B - 2, 0, False)

        def w_steps(eng, step):
            step(0, 0, 0)
            with eng.Fori(0, (NB - 4) // 2) as j:
                step(j * 2 + 1, 1, j)
                step(j * 2 + 2, 0, j + 1)
            for n in range(NB - 3, NB):
                step(n, n % 2, n // 2)

        def hold(eng, s, value):
            eng.wait_ge(s, value)
            if not isinstance(value, int):
                eng.sem_inc(s_held, 1)

        block = stack.enter_context(nc.Block())

        @block.sync
        def _(sp):
            def load_ctx(b, t):
                sp.dma_start(raw[0:ROWS[t], t, :], ctx_in[b, FIRST[t]:FIRST[t] + ROWS[t], :]).then_inc(s_raw[t], 16)

            sp.dma_start(gates[:, 0:1], g_xattn.partition_broadcast(P)).then_inc(s_const, 16)
            sp.dma_start(gates[:, 1:2], g_ffn.partition_broadcast(P)).then_inc(s_const, 16)
            sp.dma_start(xa[0:R, :], x[0]).then_inc(s_xa, 16)
            for t in range(NT):
                load_ctx(0, t)
            sp.wait_ge(s_qrows, 1)
            sp.dma_start(xa[0:R, :], x[1]).then_inc(s_xa, 16)
            for t in range(NT):
                sp.wait_ge(s_lo, t + 1)
                load_ctx(1, t)
            sp.dma_start(sn[:, :], wscale.rearrange("(t p) o -> p (t o)", p=P), allow_slow_non_contiguous=True).then_inc(s_const, 16)
            sp.dma_start(bn[:, :], wbias.rearrange("(t p) -> p t", p=P), allow_slow_non_contiguous=True).then_inc(s_const, 16)

            sp.wait_ge(s_qrows, 2)
            sp.dma_start(xa[0:R, :], x[2]).then_inc(s_xa, 16)

            def next_ctx(b):
                for t in range(NT):
                    sp.wait_ge(s_lo, b * NT + (t + 1 - NT))
                    load_ctx(b, t)

            next_ctx(2)
            with sp.Fori(3, B) as b:
                next_ctx(b)
                sp.wait_ge(s_frows, b - 2)
                sp.dma_start(xa[0:R, :], x[b]).then_inc(s_xa, 16)
            sp.wait_ge(s_pvn, NCH * (B - 1))
            for n in range(2):
                sp.dma_start(wraw[:, n, :], qweight[n * P:(n + 1) * P, :]).then_inc(s_w[n], 16)
            sp.dma_start(cB[0:R, :], wzero.rearrange("n o -> (n o)").partition_broadcast(R)).then_inc(s_bc, 16)
            sp.wait_ge(s_scores, 2 * B)
            sp.dma_start(scB[0:R, :], wscale.rearrange("n o -> (n o)").partition_broadcast(R)).then_inc(s_bc, 16)
            sp.wait_ge(s_xTfree, 16 * B)
            for b in range(B - 1):
                sp.dma_start(xT_words[:, b, :], xT_dram[b]).then_inc(s_xTin, 16)
            sp.wait_ge(s_x1out, 16 * B)
            sp.wait_ge(s_frows, B)
            sp.wait_ge(s_pvn, NCH * B)
            for b in range(B):
                sp.dma_start(x1f[0:R, b, :], x1_dram[b]).then_inc(s_x1in, 16)

            def w_step(n, par, k):
                if not isinstance(n, int) or n + 2 < NB:
                    sp.wait_ge(s_u, n + 1)
                    sp.dma_start(wraw[:, par, :], qweight[bass.ds((n + 2) * P, P), :]).then_inc(s_w[par], 16)
                if not (isinstance(n, int) and n == 0):
                    sp.wait_ge(s_add, n * 2)
                    store(n - 1)

            def store(n):
                sp.dma_start(out.rearrange("b r n -> r b n")[:, :, bass.ds(n * P, P)],
                             x1f[0:R, :, bass.ds(n * P, P)]).then_inc(s_out, 16)

            w_steps(sp, w_step)
            sp.wait_ge(s_add, 2 * NB)
            store(NB - 1)
            sp.wait_ge(s_out, 16 * NB)

        @block.gpsimd
        def _(pool):
            pool.memset(ident[:, :], 0.0).then_inc(s_id0, 1)
            pool.memset(ident16[:, :], 0.0).then_inc(s_id0, 1)
            pool.memset(half[:, :], -0.5).then_inc(s_half, 1)
            pool.wait_ge(s_id0, 2)
            for m in (ident, ident16):
                pool.affine_select(out=m[:, :], in_=m[:, :], compare_op=ALU.not_equal, fill=1.0,
                                   base=0, pattern=[[-1, P]], channel_multiplier=1).then_inc(s_id, 1)
            pool.wait_ge(s_half, 1)

            def rstd(q):
                vt, y0, a, c = (ln[0:R, k:k + 1] for k in range(4))
                hold(pool, s_aggr, q + 1)
                pool.tensor_scalar(vt, mr[0:R, 1:2], EPS, None, ALU.add).then_inc(s_var, 1)
                hold(pool, s_var, q + 1)
                pool.tensor_tensor(y0, vt, half[0:R, :], ALU.pow).then_inc(s_pow, 1)
                hold(pool, s_pow, q + 1)
                pool.tensor_tensor(a, y0, y0, ALU.mult).then_inc(s_nt, 1)
                hold(pool, s_nt, q * 3 + 1)
                pool.tensor_tensor(a, a, vt, ALU.mult).then_inc(s_nt, 1)
                hold(pool, s_nt, q * 3 + 2)
                pool.tensor_scalar(c, a, -0.5 * X_SCALE, 1.5 * X_SCALE, ALU.mult, ALU.add).then_inc(s_nt, 1)
                hold(pool, s_nt, q * 3 + 3)
                pool.tensor_tensor(mr[0:R, 1:2], y0, c, ALU.mult).then_inc(s_rstd, 1)

            def row_lo(q, src, rows_done):
                hold(pool, s_xhi, q + 1)
                pool.tensor_tensor(rows16[0:R, :, LO], src[0:R, :], rows16[0:R, :, HI], ALU.subtract).then_inc(rows_done, 1)

            def all_max(b):
                hold(pool, s_amp, b + 1)
                pool.partition_all_reduce(sc[:, 1:2], sc[:, 0:1], P, bass.bass_isa.ReduceOp.max).then_inc(s_amall, 1)

            def x1_out(i):
                hold(pool, s_x1, i * NCH + NCH)
                pool.dma_start(x1_dram[i], xres[0:R, :]).then_inc(s_x1out, 16)

            def x_in(i):
                hold(pool, s_x1out, i * 16)
                pool.dma_start(xres[0:R, :], x[i]).then_inc(s_xres, 16)

            for b in range(2):
                rstd(b)
                row_lo(b, xa, s_qrows)
                all_max(b)
            pool.dma_start(xres[0:R, :], x[0]).then_inc(s_xres, 16)
            with pool.Fori(0, B - 2) as i:
                rstd(i * 2 + 2)
                all_max(i + 2)
                row_lo(i * 2 + 2, xa, s_qrows)
                x1_out(i)
                rstd(i * 2 + 3)
                row_lo(i * 2 + 3, xa, s_frows)
                x_in(i + 1)
            x1_out(B - 2)
            rstd(LN2_6)
            row_lo(LN2_6, xa, s_frows)
            x_in(LAST)
            x1_out(LAST)
            rstd(LN2_7)
            row_lo(LN2_7, xa, s_frows)

        @block.scalar
        def _(act):
            def hi(b, par, t):
                n = ROWS[t]
                act.wait_ge(s_scale, b + 1)
                act.activation(pair[0:n, par * NT + t, :, HI], raw[0:n, t, :], ACT.Copy,
                               scale=sc2[0:n, par, 0:1]).then_inc(s_hi, 1)

            def row_hi(q, src):
                act.wait_ge(s_xn, q + 1)
                act.activation(rows16[0:R, :, HI], src[0:R, :], ACT.Copy).then_inc(s_xhi, 1)

            def turned(k, u):
                act.wait_ge(s_turned[k], u + 1)

            def ring_out(g, c):
                k, u = chunk_use(g, c)
                turned(k, u)
                act.activation(ring[:, c % RING, :], turn[k][:, 0:GW], ACT.Copy).then_inc(s_evac[k], 1)

            def rows_out(u0, dst):
                for m in range(2 * QU):
                    turned(m % 2, u0 + m // 2)
                    c0 = m * QPB * R
                    act.activation(dst[:, c0:c0 + QPB * R], turn[m % 2][:, 0:QPB * R], ACT.Copy).then_inc(s_evac[m % 2], 1)

            def probs(i, par):
                act.wait_ge(s_kneg, i + 1)
                act.activation(E[0:R, :, :], S[0:R, par, :, 0:GW], ACT.Exp, bias=soft[0:R, 1:2],
                               scale=sc2[0:R, par, 1:2], accum_out=soft[0:R, 2:3]).then_inc(s_exp, 1)

            def prob_hi(i):
                act.wait_ge(s_exp, i + 1)
                act.activation(prob16[0:R, :, HI], E[0:R, :, :].rearrange("p g k -> p (g k)"), ACT.Copy,
                               scale=P_SCALE).then_inc(s_phi, 1)

            def pT_out(u):
                for k in range(2):
                    turned(k + 2, u)
                    act.activation(pT[:, 3 * k:3 * k + 2, :], turn[k + 2][:, 0:2 * R].rearrange("p (t r) -> p t r", r=R), ACT.Copy)
                    act.activation(pT[0:ROWS[2], 3 * k + 2, :], turn[k + 2][0:ROWS[2], 2 * R:3 * R], ACT.Copy).then_inc(s_evac[k + 2], 1)

            act.sem_inc(s_xTfree, 16)
            act.wait_ge(s_const, 32)
            act.activation(tg[:, 0:2], gates[:, :], ACT.Tanh).then_inc(s_tanh, 1)
            row_hi(0, xa)
            u = Uses(0, 0)
            rows_out(u.take(QU), qT[:, 0, :])
            for t in range(3):
                hi(0, 0, t)
            g = u.group()
            for c in range(CH):
                ring_out(g, c)
                if c in (1, 4, 7):
                    hi(0, 0, 3 + c // 3)
            row_hi(1, xa)
            g = u.group()
            for c in range(CH):
                ring_out(g, c)
                if c in (8, 10, 12):
                    hi(1, 1, (8, 10, 12).index(c))
            rows_out(u.take(QU), qT[:, 1, :])
            g = u.group()
            for c in range(CH):
                ring_out(g, c)
                if c in (1, 4, 7):
                    hi(1, 1, 3 + c // 3)
            probs(0, 0)
            prob_hi(0)
            pT_out(u.take_high(1))

            def step(i, par, full):
                u = step_uses(i)
                if full:
                    for t in range(NT - 1):
                        act.wait_ge(s_pvt, i * (NT - 1) + (t + 1))
                        hi(i + 2, par, t)
                        if t == 1:
                            row_hi(ln_first(i), xa)
                    rows_out(u.take(QU), qT[:, par, :])
                g = u.group()
                for c in range(CH):
                    ring_out(g, c)
                    if full and c == HI_AT:
                        act.wait_ge(s_pvn, i * NCH + NCH)
                        hi(i + 2, par, NT - 1)
                    if full and c == ROWS_AT:
                        row_hi(ln_first(i) + 1, xa)
                if full:
                    g = u.group()
                    for c in range(CH):
                        ring_out(g, c)
                        if c == PROBS_AT:
                            probs(i + 1, 1 - par)
                        if c == PHI_AT:
                            prob_hi(i + 1)
                else:
                    probs(i + 1, 1 - par)
                    prob_hi(i + 1)
                    row_hi(LN2_6, xa)
                pT_out(u.take_high(1))
                act.wait_ge(s_xTfree, i * 16 + 16)
                c = u.take(QU)
                rows_out(c, xTst)
                for k in range(2):
                    hold(act, s_evac[k], c + QU)
                act.dma_start(xT_dram[i], xTst[:, :]).then_inc(s_xTfree, 16)

            unrolled(act, step)

            def w_out(n, par):
                turned(0, w_use(n))
                act.activation(wT[:, par, 0:HALF, :], turn[0][:, :].bitcast(F16).rearrange("p (c n) -> p c n", n=P),
                               ACT.Copy, bias=-float(BIAS16)).then_inc(s_evac[0], 1)

            w_out(0, 0)
            row_hi(LN2_7, xa)
            rows_out(C_LAST, xT_words[:, LAST, :])
            act.wait_ge(s_coefs, 1)

            def w_step(n, par, k):
                if not isinstance(n, int) or n + 1 < NB:
                    w_out(n + 1, 1 - par)
                for h in range(2):
                    hold(act, s_y, n * 2 + (h + 1))
                    act.activation(yT[:, h, :], Y[h][:, 0:HR], ACT.Identity, scale=sn[:, bass.ds(n, 1)],
                                   bias=bn[:, bass.ds(n, 1)]).then_inc(s_yev, 1)
                    if isinstance(n, int) and n == 0:
                        if h == 0:
                            act.wait_ge(s_x1in, 16 * B)
                            act.wait_ge(s_negm, 1)
                        for b in (range(0, 2), range(2, HB))[h]:
                            if b > 0:
                                act.wait_ge(s_rsA, b)
                            act.activation(junk[0:R, 0, :], x1f[0:R, b, :], ACT.Identity, bias=negm[0:R, b:b + 1],
                                           accum_out=rsum[0:R, b:b + 1]).then_inc(s_rsA, 1)

            w_steps(act, w_step)

        @block.vector
        def _(dve):
            def amax(b, t):
                dve.wait_ge(s_raw[t], b * 16 + 16)
                dve.tensor_reduce(am[0:ROWS[t], t:t + 1], raw[0:ROWS[t], t, :], AX.X, ALU.max,
                                  apply_absolute_value=True).then_inc(s_am, 1)

            def part_max(b):
                dve.wait_ge(s_am, b * NT + NT)
                dve.tensor_reduce(sc[:, 0:1], am[:, :], AX.X, ALU.max).then_inc(s_amp, 1)

            def scales(b, par):
                dve.wait_ge(s_amall, b + 1)
                dve.tensor_scalar(sc[:, 2:3], sc[:, 1:2], TINY, None, ALU.max).then_inc(s_clamp, 1)
                dve.wait_ge(s_clamp, b + 1)
                dve.tensor_scalar(sc[:, 3:4].bitcast(I32), sc[:, 2:3].bitcast(I32), 0x7F800000, None,
                                  ALU.bitwise_and).then_inc(s_pow2, 1)
                dve.wait_ge(s_pow2, b + 1)
                dve.reciprocal(sc2[:, par, 3:4], sc[:, 3:4]).then_inc(s_inv, 1)
                dve.tensor_scalar(sc2[:, par, 1:2], sc[:, 3:4], 1.0 / (C_TOP * X_SCALE), None, ALU.mult)
                dve.tensor_scalar(sc2[:, par, 2:3], sc[:, 3:4], 1.0 / (C_TOP * P_SCALE), None, ALU.mult)
                dve.wait_ge(s_inv, b + 1)
                dve.tensor_scalar(sc2[:, par, 0:1], sc2[:, par, 3:4], C_TOP, None, ALU.mult).then_inc(s_scale, 1)

            def lo(b, par, t):
                n = ROWS[t]
                dve.wait_ge(s_hi, b * NT + (t + 1))
                dve.scalar_tensor_tensor(out=pair[0:n, par * NT + t, :, LO], in0=raw[0:n, t, :],
                                         scalar=sc2[0:n, par, 0:1], in1=pair[0:n, par * NT + t, :, HI],
                                         op0=ALU.mult, op1=ALU.subtract).then_inc(s_lo, 1)

            def row_stats(q, src):
                for k in range(NCH):
                    dve.bn_stats(stats[0:R, k, :], src[0:R, k * 512:(k + 1) * 512]).then_inc(s_stat, 1)
                hold(dve, s_stat, q * NCH + NCH)
                if not (isinstance(q, int) and q == 0):
                    hold(dve, s_xn, q)
                dve.bn_aggr(mr[0:R, 0:2], stats[0:R, :, :].rearrange("p a b -> p (a b)")).then_inc(s_aggr, 1)

            def row_norm(q, rows_in):
                dve.wait_ge(s_rstd, q + 1)
                dve.tensor_scalar(xa[0:R, :], rows_in[0:R, :], mr[0:R, 0:1], mr[0:R, 1:2], ALU.subtract,
                                  ALU.mult).then_inc(s_xn, 1)

            def keep(i):
                dve.tensor_copy(mrall[0:R, bass.ds(i, 1), :], mr[0:R, 0:2].rearrange("p (o c) -> p o c", o=1)).then_inc(s_keep, 1)

            def row_max(i, par):
                dve.wait_ge(s_scores, i * 2 + 2)
                dve.tensor_reduce(soft[0:R, 0:1], S[0:R, par, :, 0:GW], AX.XY, ALU.max, negate=True).then_inc(s_nmax, 1)
                dve.wait_ge(s_nmax, i + 1)
                dve.tensor_scalar(soft[0:R, 1:2], soft[0:R, 0:1], sc2[0:R, par, 1:2], None, ALU.mult).then_inc(s_kneg, 1)

            def prob_lo(i, par):
                dve.wait_ge(s_phi, i + 1)
                dve.scalar_tensor_tensor(out=prob16[0:R, :, LO], in0=E[0:R, :, :].rearrange("p g k -> p (g k)"), scalar=P_SCALE,
                                         in1=prob16[0:R, :, HI], op0=ALU.mult, op1=ALU.subtract).then_inc(s_plo, 1)
                dve.reciprocal(soft[0:R, 3:4], soft[0:R, 2:3]).then_inc(s_rcp, 1)
                dve.wait_ge(s_rcp, i + 1)
                dve.tensor_scalar(soft[0:R, 4:5], soft[0:R, 3:4], sc2[0:R, par, 2:3], tg[0:R, 0:1], ALU.mult,
                                  ALU.mult).then_inc(s_coef, 1)

            def x1_piece(i, n):
                if n == 0:
                    dve.wait_ge(s_coef, i + 1)
                    dve.wait_ge(s_xres, i * 16 + 16)
                dve.wait_ge(s_pvn, i * NCH + (n + 1))
                piece = xres[0:R, n * 512:(n + 1) * 512]
                dve.scalar_tensor_tensor(out=piece, in0=turn[n][0:R, :], scalar=soft[0:R, 4:5], in1=piece,
                                         op0=ALU.mult, op1=ALU.add).then_inc(s_x1, 1)

            dve.memset(am[:, :], 0.0).then_inc(s_am0, 1)
            dve.wait_ge(s_xa, 16)
            row_stats(0, xa)
            dve.wait_ge(s_am0, 1)
            for t in range(NT):
                amax(0, t)
                if t == 0:
                    row_norm(0, xa)
            part_max(0)
            scales(0, 0)
            for t in range(NT):
                lo(0, 0, t)
            dve.wait_ge(s_xa, 32)
            row_stats(1, xa)
            for t in range(NT):
                amax(1, t)
                if t == 0:
                    row_norm(1, xa)
            part_max(1)
            scales(1, 1)
            for t in range(3):
                lo(1, 1, t)
            for t in range(3, NT):
                lo(1, 1, t)
            dve.wait_ge(s_tanh, 1)
            dve.tensor_scalar(tg[:, 2:3], tg[:, 1:2], 1.0 / X_SCALE, None, ALU.mult).then_inc(s_tgq, 1)
            dve.wait_ge(s_const, 64)
            dve.wait_ge(s_tgq, 1)
            dve.tensor_scalar(sn[:, :], sn[:, :], tg[:, 2:3], None, ALU.mult)
            dve.tensor_scalar(bn[:, :], bn[:, :], tg[:, 1:2], None, ALU.mult).then_inc(s_coefs, 1)

            def step(i, par, full):
                def next_amax(*tiles):
                    if full:
                        for t in tiles:
                            amax(i + 2, t)

                next_amax(0, 1)
                row_max(i, par)
                next_amax(2)
                prob_lo(i, par)
                if full:
                    dve.wait_ge(s_xa, i * 16 + 48)
                    row_stats(ln_first(i), xa)
                next_amax(3, 4, 5)
                if full:
                    part_max(i + 2)
                    scales(i + 2, par)
                    row_norm(ln_first(i), xa)
                    for t in range(3):
                        lo(i + 2, par, t)
                for n in range(NCH):
                    x1_piece(i, n)
                q = ln_first(i) + 1 if full else LN2_6
                dve.wait_ge(s_x1, i * NCH + NCH)
                row_stats(q, xres)
                if full:
                    for t in range(3, NT):
                        lo(i + 2, par, t)
                row_norm(q, xres)
                keep(i)

            unrolled(dve, step)

            def unpack(n, par, k):
                dve.wait_ge(s_w[par], k * 16 + 16)
                p = wraw[:, par, :].bitcast(U16).rearrange("p (g w h) -> p g w h", w=3, h=2)
                dve.tensor_scalar(unp[:, par, 1, :], p[:, :, 0, 0], 6, 63, ALU.logical_shift_right,
                                  ALU.bitwise_and).then_inc(s_u1, 1)
                for j, w in ((0, 0), (2, 1), (3, 2)):
                    dve.tensor_scalar(unp[:, par, j, :], p[:, :, w, 0], 63, 0x6400, ALU.bitwise_and, ALU.bitwise_or)
                dve.wait_ge(s_u1, n + 1)
                dve.tensor_scalar(unp[:, par, 1, :], unp[:, par, 1, :], 0x6400, None, ALU.bitwise_or).then_inc(s_u, 1)

            def w_out(n, par):
                dve.wait_ge(s_turned[1], w_use(n) + 1)
                dve.tensor_scalar(wT[:, par, HALF:CH, :], turn[1][:, :].bitcast(F16).rearrange("p (c n) -> p c n", n=P),
                                  -float(BIAS16), None, ALU.add).then_inc(s_evac[1], 1)

            row_max(LAST, LAST % 2)
            prob_lo(LAST, LAST % 2)
            for n in range(2):
                unpack(n, n, 0)
            for n in range(NCH):
                x1_piece(LAST, n)
            dve.wait_ge(s_x1, NCH * B)
            row_stats(LN2_7, xres)
            w_out(0, 0)
            row_norm(LN2_7, xres)
            keep(LAST)
            dve.wait_ge(s_keep, B)
            dve.tensor_scalar(negm[0:R, :], mrall[0:R, :, 0], -1.0, None, ALU.mult).then_inc(s_negm, 1)
            dve.wait_ge(s_bc, 32)
            dve.tensor_scalar(cB[0:R, :], cB[0:R, :], -1.0, 32.0, ALU.mult, ALU.add).then_inc(s_zp, 1)
            dve.wait_ge(s_zp, 1)
            dve.scalar_tensor_tensor(out=cB[0:R, :], in0=cB[0:R, :], scalar=tg[0:R, 2:3], in1=scB[0:R, :],
                                     op0=ALU.mult, op1=ALU.mult).then_inc(s_cB, 1)

            def row_sums():
                dve.wait_ge(s_x1in, 16 * B)
                for b in range(HB, B):
                    if b > HB:
                        dve.wait_ge(s_rsD, b - HB)
                    dve.tensor_scalar(junk[0:R, 1, :], x1f[0:R, b, :], mrall[0:R, b, 0:1], 0.0, ALU.subtract, ALU.add,
                                      accum_out=rsum[0:R, b:b + 1]).then_inc(s_rsD, 1)
                dve.wait_ge(s_rsD, HB)
                dve.wait_ge(s_rsA, HB)
                dve.tensor_tensor(rs8[0:R, :], rsum[0:R, :], mrall[0:R, :, 1], ALU.mult).then_inc(s_rs8, 1)
                dve.wait_ge(s_rs8, 1)
                dve.wait_ge(s_cB, 1)

            def rank_one(n):
                cols = bass.ds(n * P, P)
                for b in range(B):
                    last = dve.scalar_tensor_tensor(out=x1f[0:R, b, cols], in0=cB[0:R, cols], scalar=rs8[0:R, b:b + 1],
                                                    in1=x1f[0:R, b, cols], op0=ALU.mult, op1=ALU.add)
                last.then_inc(s_r1, 1)

            def add_up(n, h):
                dve.wait_ge(s_yb, n * 2 + (h + 1))
                block_of = x1f[0:R, h * HB:(h + 1) * HB, bass.ds(n * P, P)]
                dve.tensor_tensor(block_of, BACK[h][0:R, :].rearrange("p (b n) -> p b n", b=HB), block_of,
                                  ALU.add).then_inc(s_add, 1)

            def w_step(n, par, k):
                first = isinstance(n, int) and n == 0
                if not isinstance(n, int) or n + 1 < NB:
                    w_out(n + 1, 1 - par)
                if not isinstance(n, int) or n + 2 < NB:
                    unpack(n + 2, par, k + 1)
                if first:
                    row_sums()
                if not first:
                    add_up(n - 1, 1)
                rank_one(n)
                dve.wait_ge(s_r1, n + 1)
                add_up(n, 0)

            w_steps(dve, w_step)
            add_up(NB - 1, 1)

        @block.tensor
        def _(pe):
            def free(k, u):
                if not (isinstance(u, int) and u == 0):
                    pe.wait_ge(s_evac[k], u)

            def turn_rows(u0, ready, b, columns, attended=lambda bank: None):
                pe.wait_ge(ready, b + 1)
                for m in range(2 * QU):
                    free(m % 2, u0 + m // 2)
                    if m < 2:
                        attended(m)
                    for k in range(QPB):
                        last = pe.transpose(turn[m % 2][:, k * R:(k + 1) * R], columns(m * QPB + k), ident[0:R, 0:R])
                    last.then_inc(s_turned[m % 2], 1)

            def q_cols(c):
                return rows[0:R, c * P:(c + 1) * P]

            def ffn_cols(c):
                j, gb = divmod(c, G4 // P)
                return rows[0:R, 4 * gb * P + j:4 * (gb + 1) * P:4]

            def score_group(b, par, g, u0, attended=lambda bank: None):
                pe.wait_ge(s_lo, b * NT + (3 * g + 3))
                for c in range(CH + 4):
                    if c < CH:
                        bank, use = chunk_use(u0, c)
                        free(bank, use)
                        if c < 4:
                            attended(bank)
                        for t in range(3):
                            n = ROWS[3 * g + t]
                            last = pe.transpose(turn[bank][:, t * P:t * P + n],
                                                pair_words[0:n, par * NT + 3 * g + t, c * P:(c + 1) * P],
                                                ident[0:n, 0:n])
                        last.then_inc(s_turned[bank], 1)
                    if c >= 4:
                        m = c - 4
                        bank, use = chunk_use(u0, m)
                        pe.wait_ge(s_evac[bank], use + 1)
                        for k, (a, e) in enumerate(((HI, HI), (HI, LO), (LO, HI))):
                            last = pe.matmul(S[0:R, par, g, 0:GW], qT16[:, par, m, :, a], ring16[:, m % RING, :, e],
                                             start=(m == 0 and k == 0), stop=(m == CH - 1 and k == 2))
                last.then_inc(s_scores, 1)

            def turn_probs(i, u):
                pe.wait_ge(s_plo, i + 1)
                for t in range(NT):
                    k = 2 + t // 3
                    if t % 3 == 0:
                        free(k, u)
                    n = ROWS[t]
                    last = pe.transpose(turn[k][0:n, (t % 3) * R:(t % 3 + 1) * R], prob[0:R, FIRST[t]:FIRST[t] + n],
                                        ident[0:R, 0:R])
                    if t % 3 == 2:
                        last.then_inc(s_turned[k], 1)

            def probs_turned(u):
                for k in (2, 3):
                    pe.wait_ge(s_evac[k], u + 1)

            def attend(i, par, low, high):
                for t in range(NT):
                    r = ROWS[t]
                    for n in (0, 1, 2, 3) if t else (2, 3, 0, 1):
                        if t == 0:
                            free(n, high if n > 1 else low)
                        for k, (a, e) in enumerate(((HI, HI), (HI, LO), (LO, HI))):
                            last = pe.matmul(turn[n][0:R, :], pT16[0:r, t, :, a],
                                             pair[0:r, par * NT + t, n * 512:(n + 1) * 512, e],
                                             start=(t == 0 and k == 0), stop=(t == NT - 1 and k == 2))
                        if t == NT - 1:
                            last.then_inc(s_pvn, 1)
                    if t < NT - 1:
                        last.then_inc(s_pvt, 1)

            pe.wait_ge(s_id, 2)
            u = Uses(0, 0)
            turn_rows(u.take(QU), s_qrows, 0, q_cols)
            score_group(0, 0, 0, u.group())
            score_group(0, 0, 1, u.group())
            turn_rows(u.take(QU), s_qrows, 1, q_cols)
            score_group(1, 1, 0, u.group())
            probs = u.take_high(1)
            turn_probs(0, probs)
            probs_turned(probs)

            def step(i, par, full):
                u = step_uses(i)
                attend(i, par, u.take(0), u.take_high(0))

                def attended(bank):
                    pe.wait_ge(s_x1, i * NCH + (bank + 1))

                if full:
                    turn_rows(u.take(QU), s_qrows, i + 2, q_cols, attended)
                score_group(i + 1, 1 - par, 1, u.group(), attended)
                if full:
                    score_group(i + 2, par, 0, u.group())
                probs = u.take_high(1)
                turn_probs(i + 1, probs)
                turn_rows(u.take(QU), s_frows, i, ffn_cols)
                probs_turned(probs)

            unrolled(pe, step)

            def turn_weights(n, par):
                pe.wait_ge(s_u, n + 1)
                for c in range(CH):
                    if c % HALF == 0:
                        free(c // HALF, w_use(n))
                    j, gb = divmod(c, G4 // P)
                    last = pe.transpose(turn[c // HALF][:, :].bitcast(F16)[:, (c % HALF) * P:(c % HALF + 1) * P],
                                        unp[:, par, j, gb * P:(gb + 1) * P].bitcast(F16), ident16[:, :])
                    if c % HALF == HALF - 1:
                        last.then_inc(s_turned[c // HALF], 1)

            def multiply(n, par, h):
                if not (isinstance(n, int) and n == 0):
                    pe.wait_ge(s_yev, n * 2 + (h - 1))
                for c in range(CH):
                    for k in (HI, LO):
                        last = pe.matmul(Y[h][:, 0:HR], wT[:, par, c, :], xTv[:, h * HB:(h + 1) * HB, c, :, k],
                                         start=(c == 0 and k == HI), stop=(c == CH - 1 and k == LO))
                last.then_inc(s_y, 1)

            def turn_back(n, h):
                pe.wait_ge(s_yev, n * 2 + (h + 1))
                if not (isinstance(n, int) and n == 0):
                    pe.wait_ge(s_add, n * 2 + (h - 1))
                for b in range(HB):
                    last = pe.transpose(BACK[h][0:R, b * P:(b + 1) * P], yT[:, h, b * R:(b + 1) * R], ident[:, :])
                last.then_inc(s_yb, 1)

            attend(LAST, LAST % 2, W_USE, PRO[1] + LAST * STEP[1] - GU)
            for n in range(NCH):
                pe.wait_ge(s_x1, LAST * NCH + (n + 1))
            turn_weights(0, 0)
            turn_rows(C_LAST, s_frows, LAST, ffn_cols)
            pe.wait_ge(s_xTin, 16 * (B - 1))

            def w_step(n, par, k):
                for q in range(2):
                    pe.wait_ge(s_evac[q], w_use(n) + 1 if not (isinstance(n, int) and n == 0) else C_LAST + QU)
                if not isinstance(n, int) or n + 1 < NB:
                    turn_weights(n + 1, 1 - par)
                multiply(n, par, 0)
                if not (isinstance(n, int) and n == 0):
                    turn_back(n - 1, 1)
                multiply(n, par, 1)
                turn_back(n, 0)

            w_steps(pe, w_step)
            turn_back(NB - 1, 1)


_INS = ["x", "ctx_4096", "g_xattn", "g_ffn", "L0_ffn_qweight", "L0_ffn_weight_scale", "L0_ffn_weight_zero_point", "L0_ffn_bias"]


def kernel(**inputs):
    import numpy as np
    import concourse.bacc as bacc
    from concourse.bass_utils import run_bass_kernel_spmd

    nc = bacc.Bacc("TRN2", target_bir_lowering=False, num_devices=1)
    arrays, args = {}, []
    for name in _INS:
        a = np.ascontiguousarray(inputs[name])
        arrays[f"in_{name}"] = a
        args.append(nc.dram_tensor(f"in_{name}", a.shape, mybir.dt.from_np(a.dtype), kind="ExternalInput").ap())
    shape = np.asarray(inputs["x"]).shape
    args.append(nc.dram_tensor("out_y", shape, F32, kind="ExternalOutput").ap())
    flamingo_block(nc, *args)
    r = run_bass_kernel_spmd(nc, [arrays], core_ids=[0])
    return r.results[0]["out_y"]
```

```python
from contextlib import ExitStack

import concourse.bass as bass
from concourse import mybir

F32 = mybir.dt.float32
F16 = mybir.dt.float16
I32 = mybir.dt.int32
U16 = mybir.dt.uint16
ALU = mybir.AluOpType
ACT = mybir.ActivationFunctionType
AX = mybir.AxisListType

HI, LO = 1, 0
EPS = 1e-5
X_SCALE = 256.0
P_SCALE = 4096.0
C_TOP = 2.0 ** 14
BIAS16 = 1024 + 32
TINY = 2.0 ** -100


def flamingo_block(nc, x, ctx_in, g_xattn, g_ffn, qweight, wscale, wzero, wbias, out):
    B, R, D = x.shape
    K = ctx_in.shape[1]
    N, WP = qweight.shape
    P = 128
    CH = D // P
    GW = K // 2
    assert K % 2 == 0 and GW <= 512 and R <= P
    ROWS = [P, P, GW - 2 * P] * 2
    FIRST = [0, P, 2 * P, GW, GW + P, GW + 2 * P]
    NT = len(ROWS)
    NCH = D // 512
    NB = N // P
    G4 = D // 4
    HB = B // 2
    HR = HB * R
    RING = 8
    QPB = P // 32

    with ExitStack() as stack:
        def sb(name, shape, dt=F32):
            return stack.enter_context(nc.sbuf_tensor(name, shape, dt))

        def psum(name):
            return stack.enter_context(nc.psum_tensor(name, [P, 512], F32))

        def sem(name):
            return stack.enter_context(nc.semaphore(name))

        x1_dram = nc.dram_tensor("x1_scratch", (B, R, D), F32, kind="Internal").ap()
        xT_dram = nc.dram_tensor("xT_scratch", (B, P, CH * R), F32, kind="Internal").ap()

        arena = sb("arena", [P, 2 * NT * D + 2 * D + NT * D + RING * GW])
        at = [0]

        def cut(words):
            at[0] += words
            return arena[:, at[0] - words:at[0]]

        pair = cut(2 * NT * D).bitcast(F16).rearrange("p (s d h) -> p s d h", s=2 * NT, h=2)
        xa = cut(D)
        xres = cut(D)
        raw = cut(NT * D).rearrange("p (t d) -> p t d", t=NT)
        ring = cut(RING * GW).rearrange("p (s k) -> p s k", s=RING)
        pair_words = arena[:, 0:2 * NT * D].rearrange("p (s d) -> p s d", s=2 * NT)
        at[0] = 0
        wraw = cut(2 * WP).bitcast(I32).rearrange("p (s w) -> p s w", s=2)
        unp = cut(D).bitcast(U16).rearrange("p (s j g) -> p s j g", s=2, j=4)
        wT = cut(D).bitcast(F16).rearrange("p (s c n) -> p s c n", s=2, c=CH)
        yT = cut(2 * HR).rearrange("p (h r) -> p h r", h=2)
        cB = cut(N)
        assert at[0] <= NT * D
        at[0] = NT * D
        x1f = cut(B * D).rearrange("p (b d) -> p b d", b=B)
        xT = cut(B * CH * R)
        xT_words = xT.rearrange("p (b w) -> p b w", b=B)
        xTv = xT.bitcast(F16).rearrange("p (b c r h) -> p b c r h", b=B, c=CH, h=2)
        scB = cut(N)
        assert at[0] <= 3 * NT * D + 2 * D + RING * GW
        assert (B - 1) * D == NT * D + D and B * CH * R - CH * R <= NT * D

        rows = sb("rows", [P, D])
        rows16 = rows[:].bitcast(F16).rearrange("p (d h) -> p d h", h=2)
        qT = sb("qT", [P, 2, CH * R])
        qT16 = qT[:].bitcast(F16).rearrange("p s (c r h) -> p s c r h", c=CH, h=2)
        xTst = sb("xTst", [P, CH * R])
        E = sb("E", [P, 2, GW])
        prob = sb("prob", [P, K])
        prob16 = prob[:].bitcast(F16).rearrange("p (k h) -> p k h", h=2)
        pT = sb("pT", [P, NT, R])
        pT16 = pT[:].bitcast(F16).rearrange("p t (r h) -> p t r h", h=2)
        ring16 = ring.bitcast(F16).rearrange("p s (k h) -> p s k h", h=2)
        ident = sb("ident", [P, P])
        ident16 = sb("ident16", [P, P], F16)
        am = sb("am", [P, NT])
        sc = sb("sc", [P, 4])
        sc2 = sb("sc2", [P, 2, 4])
        soft = sb("soft", [P, 6])
        stats = sb("stats", [P, NCH, 6])
        mr = sb("mr", [P, 2])
        ln = sb("ln", [P, 6])
        half = sb("half", [P, 1])
        row_sum = sb("row_sum", [P, B])
        gates = sb("gates", [P, 2])
        tg = sb("tg", [P, 3])
        sn = sb("sn", [P, NB])
        bn = sb("bn", [P, NB])

        turn = [psum(f"turn{k}") for k in range(4)]
        S = stack.enter_context(nc.psum_tensor("S", [P, 2, 2, 512], F32))
        BACK = turn[2:4]
        Y = [S[:, 0, h, :] for h in range(2)]

        s_raw = [sem(f"s_raw{t}") for t in range(NT)]
        s_xa = sem("s_xa")
        s_xres = sem("s_xres")
        s_const = sem("s_const")
        s_x1out = sem("s_x1out")
        s_xTfree = sem("s_xTfree")
        s_x1in = sem("s_x1in")
        s_xTin = sem("s_xTin")
        s_bc = sem("s_bc")
        s_w = [sem(f"s_w{k}") for k in range(2)]
        s_out = sem("s_out")
        s_id0 = sem("s_id0")
        s_id = sem("s_id")
        s_am0 = sem("s_am0")
        s_am = sem("s_am")
        s_amp = sem("s_amp")
        s_amall = sem("s_amall")
        s_clamp = sem("s_clamp")
        s_pow2 = sem("s_pow2")
        s_inv = sem("s_inv")
        s_scale = sem("s_scale")
        s_hi = sem("s_hi")
        s_lo = sem("s_lo")
        s_turned = [sem(f"s_turned{k}") for k in range(4)]
        s_evac = [sem(f"s_evac{k}") for k in range(4)]
        s_scores = sem("s_scores")
        s_nmax = sem("s_nmax")
        s_kneg = sem("s_kneg")
        s_exp = sem("s_exp")
        s_phi = sem("s_phi")
        s_plo = sem("s_plo")
        s_rcp = sem("s_rcp")
        s_coef = sem("s_coef")
        s_pvn = sem("s_pvn")
        s_pvt = sem("s_pvt")
        s_x1 = sem("s_x1")
        s_stat = sem("s_stat")
        s_aggr = sem("s_aggr")
        s_var = sem("s_var")
        s_pow = sem("s_pow")
        s_nt = sem("s_nt")
        s_rstd = sem("s_rstd")
        s_xn = sem("s_xn")
        s_xhi = sem("s_xhi")
        s_qrows = sem("s_qrows")
        s_frows = sem("s_frows")
        s_half = sem("s_half")
        s_tanh = sem("s_tanh")
        s_tgq = sem("s_tgq")
        s_coefs = sem("s_coefs")
        s_u1 = sem("s_u1")
        s_u = sem("s_u")
        s_y = sem("s_y")
        s_yev = sem("s_yev")
        s_yb = sem("s_yb")
        s_zp = sem("s_zp")
        s_held = sem("s_held")
        s_cB = sem("s_cB")
        s_r1 = sem("s_r1")
        s_add = sem("s_add")

        HALF = CH // 2
        QU = CH // QPB // 2
        GU = CH // 4
        PRO = (2 * QU + 3 * GU, 3 * GU + 1)
        STEP = (2 * QU + 2 * GU, 2 * GU + 1)
        LAST = B - 1

        class Uses:

            def __init__(self, low_first, high_first):
                self.first, self.n = (low_first, high_first), [0, 0]

            def take(self, k):
                self.n[0] += k
                return self.first[0] + (self.n[0] - k)

            def take_high(self, k):
                self.n[1] += k
                return self.first[1] + (self.n[1] - k)

            def group(self):
                at = [f + n for f, n in zip(self.first, self.n)]
                self.n = [n + GU for n in self.n]
                return at

        def chunk_use(group, c):
            return c % 4, group[c % 4 // 2] + c // 4

        def step_uses(i):
            return Uses(i * STEP[0] + PRO[0], i * STEP[1] + PRO[1])

        W_USE = PRO[0] + (B - 1) * STEP[0] - QU - GU
        C_LAST = W_USE + 2

        def w_use(n):
            return n + (W_USE + QU) if not isinstance(n, int) or n > 1 else W_USE + n

        def ln_first(i):
            return i * 2 + 2

        HI_AT, ROWS_AT = 3, 13
        FIRST_HI_AT = (2, 4, 6, 9, 12, 15)
        FIRST_ROWS_AT = 0
        PROBS_AT, PHI_AT = 2, 4

        LN2_6, LN2_7 = 2 * B - 2, 2 * B - 1

        def unrolled(eng, step):
            step(0, 0, True)
            step(1, 1, True)
            with eng.Fori(1, (B - 2) // 2) as j:
                step(j * 2, 0, True)
                step(j * 2 + 1, 1, True)
            step(B - 2, 0, False)

        def w_steps(eng, step):
            step(0, 0, 0)
            with eng.Fori(0, (NB - 4) // 2) as j:
                step(j * 2 + 1, 1, j)
                step(j * 2 + 2, 0, j + 1)
            for n in range(NB - 3, NB):
                step(n, n % 2, n // 2)

        def hold(eng, s, value):
            eng.wait_ge(s, value)
            if not isinstance(value, int):
                eng.sem_inc(s_held, 1)

        block = stack.enter_context(nc.Block())

        @block.sync
        def _(sp):
            def load_ctx(b, t):
                sp.dma_start(raw[0:ROWS[t], t, :], ctx_in[b, FIRST[t]:FIRST[t] + ROWS[t], :]).then_inc(s_raw[t], 16)

            sp.dma_start(gates[:, 0:1], g_xattn.partition_broadcast(P)).then_inc(s_const, 16)
            sp.dma_start(gates[:, 1:2], g_ffn.partition_broadcast(P)).then_inc(s_const, 16)
            sp.dma_start(xa[0:R, :], x[0]).then_inc(s_xa, 16)
            for t in range(NT):
                load_ctx(0, t)
            sp.wait_ge(s_qrows, 1)
            sp.dma_start(xa[0:R, :], x[1]).then_inc(s_xa, 16)
            for t in range(NT):
                sp.wait_ge(s_lo, t + 1)
                load_ctx(1, t)
            sp.dma_start(sn[:, :], wscale.rearrange("(t p) o -> p (t o)", p=P), allow_slow_non_contiguous=True).then_inc(s_const, 16)
            sp.dma_start(bn[:, :], wbias.rearrange("(t p) -> p t", p=P), allow_slow_non_contiguous=True).then_inc(s_const, 16)

            sp.wait_ge(s_qrows, 2)
            sp.dma_start(xa[0:R, :], x[2]).then_inc(s_xa, 16)

            def next_ctx(b):
                for t in range(NT):
                    sp.wait_ge(s_lo, b * NT + (t + 1 - NT))
                    load_ctx(b, t)

            next_ctx(2)
            with sp.Fori(3, B) as b:
                next_ctx(b)
                sp.wait_ge(s_frows, b - 2)
                sp.dma_start(xa[0:R, :], x[b]).then_inc(s_xa, 16)
            sp.wait_ge(s_lo, B * NT)
            sp.wait_ge(s_xTfree, 16 * (B - 1))
            for b in range(B - 2):
                sp.dma_start(xT_words[:, b, :], xT_dram[b]).then_inc(s_xTin, 16)
            sp.wait_ge(s_pvn, NCH * (B - 1))
            for n in range(2):
                sp.dma_start(wraw[:, n, :], qweight[n * P:(n + 1) * P, :]).then_inc(s_w[n], 16)
            sp.dma_start(cB[0:R, :], wzero.rearrange("n o -> (n o)").partition_broadcast(R)).then_inc(s_bc, 16)
            sp.wait_ge(s_scores, 2 * B)
            sp.dma_start(scB[0:R, :], wscale.rearrange("n o -> (n o)").partition_broadcast(R)).then_inc(s_bc, 16)
            sp.wait_ge(s_u, 1)
            sp.dma_start(wraw[:, 0, :], qweight[2 * P:3 * P, :]).then_inc(s_w[0], 16)
            sp.wait_ge(s_xTfree, 16 * B)
            sp.dma_start(xT_words[:, B - 2, :], xT_dram[B - 2]).then_inc(s_xTin, 16)
            sp.wait_ge(s_x1out, 16 * (B - 1))
            sp.wait_ge(s_pvn, NCH * B)
            for b in range(B - 2):
                sp.dma_start(x1f[0:R, b, :], x1_dram[b]).then_inc(s_x1in, 16)
            sp.wait_ge(s_frows, B)
            sp.dma_start(x1f[0:R, B - 2, :], x1_dram[B - 2]).then_inc(s_x1in, 16)

            def w_step(n, par, k):
                if not isinstance(n, int) or 0 < n < NB - 2:
                    sp.wait_ge(s_u, n + 1)
                    sp.dma_start(wraw[:, par, :], qweight[bass.ds((n + 2) * P, P), :]).then_inc(s_w[par], 16)
                if not (isinstance(n, int) and n == 0):
                    sp.wait_ge(s_add, n * 2)
                    store(n - 1)

            def store(n):
                sp.dma_start(out.rearrange("b r n -> r b n")[:, :, bass.ds(n * P, P)],
                             x1f[0:R, :, bass.ds(n * P, P)]).then_inc(s_out, 16)

            w_steps(sp, w_step)
            sp.wait_ge(s_add, 2 * NB)
            store(NB - 1)
            sp.wait_ge(s_out, 16 * NB)

        @block.gpsimd
        def _(pool):
            pool.memset(ident[:, :], 0.0).then_inc(s_id0, 1)
            pool.memset(ident16[:, :], 0.0).then_inc(s_id0, 1)
            pool.memset(half[:, :], -0.5).then_inc(s_half, 1)
            pool.wait_ge(s_id0, 2)
            for m in (ident, ident16):
                pool.affine_select(out=m[:, :], in_=m[:, :], compare_op=ALU.not_equal, fill=1.0,
                                   base=0, pattern=[[-1, P]], channel_multiplier=1).then_inc(s_id, 1)
            pool.wait_ge(s_half, 1)

            def rstd(q):
                vt, y0, a, c = (ln[0:R, k:k + 1] for k in range(4))
                hold(pool, s_aggr, q + 1)
                pool.tensor_scalar(vt, mr[0:R, 1:2], EPS, None, ALU.add).then_inc(s_var, 1)
                hold(pool, s_var, q + 1)
                pool.tensor_tensor(y0, vt, half[0:R, :], ALU.pow).then_inc(s_pow, 1)
                hold(pool, s_pow, q + 1)
                pool.tensor_tensor(a, y0, y0, ALU.mult).then_inc(s_nt, 1)
                hold(pool, s_nt, q * 3 + 1)
                pool.tensor_tensor(a, a, vt, ALU.mult).then_inc(s_nt, 1)
                hold(pool, s_nt, q * 3 + 2)
                pool.tensor_scalar(c, a, -0.5 * X_SCALE, 1.5 * X_SCALE, ALU.mult, ALU.add).then_inc(s_nt, 1)
                hold(pool, s_nt, q * 3 + 3)
                pool.tensor_tensor(mr[0:R, 1:2], y0, c, ALU.mult).then_inc(s_rstd, 1)

            def row_lo(q, src, rows_done):
                hold(pool, s_xhi, q + 1)
                pool.tensor_tensor(rows16[0:R, :, LO], src[0:R, :], rows16[0:R, :, HI], ALU.subtract).then_inc(rows_done, 1)

            def all_max(b):
                hold(pool, s_amp, b + 1)
                pool.partition_all_reduce(sc[:, 1:2], sc[:, 0:1], P, bass.bass_isa.ReduceOp.max).then_inc(s_amall, 1)

            def x1_out(i):
                hold(pool, s_x1, i * NCH + NCH)
                pool.dma_start(x1_dram[i], xres[0:R, :]).then_inc(s_x1out, 16)

            def x_in(i):
                hold(pool, s_x1out, i * 16)
                pool.dma_start(xres[0:R, :], x[i]).then_inc(s_xres, 16)

            for b in range(2):
                rstd(b)
                row_lo(b, xa, s_qrows)
                all_max(b)
            pool.dma_start(xres[0:R, :], x[0]).then_inc(s_xres, 16)
            rstd(2)
            row_lo(2, xa, s_qrows)
            x1_out(0)
            rstd(3)
            all_max(2)
            row_lo(3, xa, s_frows)
            x_in(1)
            with pool.Fori(1, B - 2) as i:
                rstd(i * 2 + 2)
                all_max(i + 2)
                row_lo(i * 2 + 2, xa, s_qrows)
                x1_out(i)
                rstd(i * 2 + 3)
                row_lo(i * 2 + 3, xa, s_frows)
                x_in(i + 1)
            x1_out(B - 2)
            rstd(LN2_6)
            row_lo(LN2_6, xa, s_frows)
            x_in(LAST)
            rstd(LN2_7)
            row_lo(LN2_7, xa, s_frows)

        @block.scalar
        def _(act):
            def hi(b, par, t):
                n = ROWS[t]
                act.wait_ge(s_scale, b + 1)
                act.activation(pair[0:n, par * NT + t, :, HI], raw[0:n, t, :], ACT.Copy,
                               scale=sc2[0:n, par, 0:1]).then_inc(s_hi, 1)

            def row_hi(q, src):
                act.wait_ge(s_xn, q + 1)
                act.activation(rows16[0:R, :, HI], src[0:R, :], ACT.Copy).then_inc(s_xhi, 1)

            def ffn_row_hi(i, q):
                hold(act, s_xn, q + 1)
                act.activation(rows16[0:R, :, HI], xa[0:R, :], ACT.Identity,
                               accum_out=row_sum[0:R, bass.ds(i, 1)]).then_inc(s_xhi, 1)

            def turned(k, u):
                act.wait_ge(s_turned[k], u + 1)

            def ring_out(g, c):
                k, u = chunk_use(g, c)
                turned(k, u)
                act.activation(ring[:, c % RING, :], turn[k][:, 0:GW], ACT.Copy).then_inc(s_evac[k], 1)

            def rows_out(u0, dst):
                for m in range(2 * QU):
                    turned(m % 2, u0 + m // 2)
                    c0 = m * QPB * R
                    act.activation(dst[:, c0:c0 + QPB * R], turn[m % 2][:, 0:QPB * R], ACT.Copy).then_inc(s_evac[m % 2], 1)

            def probs(i, par):
                act.wait_ge(s_kneg, i + 1)
                act.activation(E[0:R, :, :], S[0:R, par, :, 0:GW], ACT.Exp, bias=soft[0:R, 1:2],
                               scale=sc2[0:R, par, 1:2], accum_out=soft[0:R, 2:3]).then_inc(s_exp, 1)

            def prob_hi(i):
                act.wait_ge(s_exp, i + 1)
                act.activation(prob16[0:R, :, HI], E[0:R, :, :].rearrange("p g k -> p (g k)"), ACT.Copy,
                               scale=P_SCALE).then_inc(s_phi, 1)

            def pT_out(u):
                for k in range(2):
                    turned(k + 2, u)
                    act.activation(pT[:, 3 * k:3 * k + 2, :], turn[k + 2][:, 0:2 * R].rearrange("p (t r) -> p t r", r=R), ACT.Copy)
                    act.activation(pT[0:ROWS[2], 3 * k + 2, :], turn[k + 2][0:ROWS[2], 2 * R:3 * R], ACT.Copy).then_inc(s_evac[k + 2], 1)

            act.sem_inc(s_xTfree, 16)
            act.wait_ge(s_const, 32)
            act.activation(tg[:, 0:2], gates[:, :], ACT.Tanh).then_inc(s_tanh, 1)
            row_hi(0, xa)
            u = Uses(0, 0)
            rows_out(u.take(QU), qT[:, 0, :])
            for t in range(3):
                hi(0, 0, t)
            g = u.group()
            for c in range(CH):
                ring_out(g, c)
                if c in (1, 4, 7):
                    hi(0, 0, 3 + c // 3)
            g = u.group()
            for c in range(CH):
                ring_out(g, c)
                if c == 8:
                    row_hi(1, xa)
            probs(0, 0)
            prob_hi(0)
            hi(1, 1, 0)
            pT_out(u.take_high(1))
            for t in range(1, NT):
                hi(1, 1, t)
            rows_out(u.take(QU), qT[:, 1, :])
            g = u.group()
            for c in range(CH):
                ring_out(g, c)
                if c == 3:
                    row_hi(2, xa)

            def step(i, par, full):
                u = step_uses(i)
                first = isinstance(i, int) and i == 0
                if first:
                    rows_out(u.take(QU), qT[:, 0, :])
                elif full:
                    for t in range(NT - 1):
                        act.wait_ge(s_pvt, i * (NT - 1) + (t + 1))
                        hi(i + 2, par, t)
                        if t == 1:
                            row_hi(ln_first(i), xa)
                    rows_out(u.take(QU), qT[:, par, :])
                g = u.group()
                for c in range(CH):
                    ring_out(g, c)
                    if first and c == FIRST_ROWS_AT:
                        ffn_row_hi(0, ln_first(0) + 1)
                    if first and c in FIRST_HI_AT:
                        act.wait_ge(s_pvn, NCH)
                        hi(2, 0, FIRST_HI_AT.index(c))
                    elif full and not first and c == HI_AT:
                        act.wait_ge(s_pvn, i * NCH + NCH)
                        hi(i + 2, par, NT - 1)
                    if c == ROWS_AT and not first:
                        ffn_row_hi(i, ln_first(i) + 1 if full else LN2_6)
                if full:
                    g = u.group()
                    for c in range(CH):
                        ring_out(g, c)
                        if c == PROBS_AT:
                            probs(i + 1, 1 - par)
                        if c == PHI_AT:
                            prob_hi(i + 1)
                else:
                    probs(i + 1, 1 - par)
                    prob_hi(i + 1)
                if full:
                    pT_out(u.take_high(1))
                act.wait_ge(s_xTfree, i * 16 + 16)
                c = u.take(QU)
                rows_out(c, xTst)
                if not full:
                    pT_out(u.take_high(1))
                    w_out(0, 0)
                for k in range(2):
                    hold(act, s_evac[k], c + QU)
                act.dma_start(xT_dram[i], xTst[:, :]).then_inc(s_xTfree, 16)

            def w_out(n, par):
                turned(0, w_use(n))
                act.activation(wT[:, par, 0:HALF, :], turn[0][:, :].bitcast(F16).rearrange("p (c n) -> p c n", n=P),
                               ACT.Copy, bias=-float(BIAS16)).then_inc(s_evac[0], 1)

            unrolled(act, step)

            def y_out(n, h):
                hold(act, s_y, n * 2 + (h + 1))
                act.activation(yT[:, h, :], Y[h][:, 0:HR], ACT.Identity, scale=sn[:, bass.ds(n, 1)],
                               bias=bn[:, bass.ds(n, 1)]).then_inc(s_yev, 1)

            w_out(1, 1)
            ffn_row_hi(LAST, LN2_7)
            act.wait_ge(s_coefs, 1)
            y_out(0, 0)
            rows_out(C_LAST, xT_words[:, LAST, :])

            def w_step(n, par, k):
                if isinstance(n, int) and n == 0:
                    y_out(0, 1)
                    return
                if not isinstance(n, int) or n + 1 < NB:
                    w_out(n + 1, 1 - par)
                y_out(n, 0)
                y_out(n, 1)

            w_steps(act, w_step)

        @block.vector
        def _(dve):
            def amax(b, t):
                dve.wait_ge(s_raw[t], b * 16 + 16)
                dve.tensor_reduce(am[0:ROWS[t], t:t + 1], raw[0:ROWS[t], t, :], AX.X, ALU.max,
                                  apply_absolute_value=True).then_inc(s_am, 1)

            def part_max(b):
                dve.wait_ge(s_am, b * NT + NT)
                dve.tensor_reduce(sc[:, 0:1], am[:, :], AX.X, ALU.max).then_inc(s_amp, 1)

            def scales(b, par):
                dve.wait_ge(s_amall, b + 1)
                dve.tensor_scalar(sc[:, 2:3], sc[:, 1:2], TINY, None, ALU.max).then_inc(s_clamp, 1)
                dve.wait_ge(s_clamp, b + 1)
                dve.tensor_scalar(sc[:, 3:4].bitcast(I32), sc[:, 2:3].bitcast(I32), 0x7F800000, None,
                                  ALU.bitwise_and).then_inc(s_pow2, 1)
                dve.wait_ge(s_pow2, b + 1)
                dve.reciprocal(sc2[:, par, 3:4], sc[:, 3:4]).then_inc(s_inv, 1)
                dve.tensor_scalar(sc2[:, par, 1:2], sc[:, 3:4], 1.0 / (C_TOP * X_SCALE), None, ALU.mult)
                dve.tensor_scalar(sc2[:, par, 2:3], sc[:, 3:4], 1.0 / (C_TOP * P_SCALE), None, ALU.mult)
                dve.wait_ge(s_inv, b + 1)
                dve.tensor_scalar(sc2[:, par, 0:1], sc2[:, par, 3:4], C_TOP, None, ALU.mult).then_inc(s_scale, 1)

            def lo(b, par, t):
                n = ROWS[t]
                dve.wait_ge(s_hi, b * NT + (t + 1))
                dve.scalar_tensor_tensor(out=pair[0:n, par * NT + t, :, LO], in0=raw[0:n, t, :],
                                         scalar=sc2[0:n, par, 0:1], in1=pair[0:n, par * NT + t, :, HI],
                                         op0=ALU.mult, op1=ALU.subtract).then_inc(s_lo, 1)

            def row_stats(q, src):
                for k in range(NCH):
                    dve.bn_stats(stats[0:R, k, :], src[0:R, k * 512:(k + 1) * 512]).then_inc(s_stat, 1)
                hold(dve, s_stat, q * NCH + NCH)
                if not (isinstance(q, int) and q == 0):
                    hold(dve, s_xn, q)
                dve.bn_aggr(mr[0:R, 0:2], stats[0:R, :, :].rearrange("p a b -> p (a b)")).then_inc(s_aggr, 1)

            def row_norm(q, rows_in):
                dve.wait_ge(s_rstd, q + 1)
                dve.tensor_scalar(xa[0:R, :], rows_in[0:R, :], mr[0:R, 0:1], mr[0:R, 1:2], ALU.subtract,
                                  ALU.mult).then_inc(s_xn, 1)

            def row_max(i, par):
                dve.wait_ge(s_scores, i * 2 + 2)
                dve.tensor_reduce(soft[0:R, 0:1], S[0:R, par, :, 0:GW], AX.XY, ALU.max, negate=True).then_inc(s_nmax, 1)
                dve.wait_ge(s_nmax, i + 1)
                dve.tensor_scalar(soft[0:R, 1:2], soft[0:R, 0:1], sc2[0:R, par, 1:2], None, ALU.mult).then_inc(s_kneg, 1)

            def prob_lo(i, par):
                dve.wait_ge(s_phi, i + 1)
                dve.scalar_tensor_tensor(out=prob16[0:R, :, LO], in0=E[0:R, :, :].rearrange("p g k -> p (g k)"), scalar=P_SCALE,
                                         in1=prob16[0:R, :, HI], op0=ALU.mult, op1=ALU.subtract).then_inc(s_plo, 1)
                dve.reciprocal(soft[0:R, 3:4], soft[0:R, 2:3]).then_inc(s_rcp, 1)
                dve.wait_ge(s_rcp, i + 1)
                dve.tensor_scalar(soft[0:R, 4:5], soft[0:R, 3:4], sc2[0:R, par, 2:3], tg[0:R, 0:1], ALU.mult,
                                  ALU.mult).then_inc(s_coef, 1)

            def x1_piece(i, n):
                if n == 0:
                    dve.wait_ge(s_coef, i + 1)
                    dve.wait_ge(s_xres, i * 16 + 16)
                dve.wait_ge(s_pvn, i * NCH + (n + 1))
                piece = xres[0:R, n * 512:(n + 1) * 512]
                dve.scalar_tensor_tensor(out=piece, in0=turn[n][0:R, :], scalar=soft[0:R, 4:5], in1=piece,
                                         op0=ALU.mult, op1=ALU.add).then_inc(s_x1, 1)

            dve.memset(am[:, :], 0.0).then_inc(s_am0, 1)
            dve.wait_ge(s_xa, 16)
            row_stats(0, xa)
            dve.wait_ge(s_am0, 1)
            for t in range(NT):
                amax(0, t)
                if t == 0:
                    row_norm(0, xa)
            part_max(0)
            scales(0, 0)
            for t in range(NT):
                lo(0, 0, t)
            dve.wait_ge(s_xa, 32)
            row_stats(1, xa)
            for t in range(NT):
                amax(1, t)
                if t == 0:
                    row_norm(1, xa)
            part_max(1)
            row_max(0, 0)
            scales(1, 1)
            dve.wait_ge(s_tanh, 1)
            prob_lo(0, 0)
            for t in range(NT):
                lo(1, 1, t)
                if t == 0:
                    dve.wait_ge(s_xa, 48)
                    row_stats(2, xa)
                if t == 2:
                    row_norm(2, xa)
            dve.tensor_scalar(tg[:, 2:3], tg[:, 1:2], 1.0 / X_SCALE, None, ALU.mult).then_inc(s_tgq, 1)
            dve.wait_ge(s_const, 64)
            dve.wait_ge(s_tgq, 1)
            dve.tensor_scalar(sn[:, :], sn[:, :], tg[:, 2:3], None, ALU.mult)
            dve.tensor_scalar(bn[:, :], bn[:, :], tg[:, 1:2], None, ALU.mult).then_inc(s_coefs, 1)

            def step(i, par, full):
                def next_amax(*tiles):
                    if full:
                        for t in tiles:
                            amax(i + 2, t)

                first = isinstance(i, int) and i == 0
                if first:
                    next_amax(0)
                    for n in range(NCH):
                        x1_piece(0, n)
                    dve.wait_ge(s_x1, NCH)
                    row_stats(ln_first(0) + 1, xres)
                    next_amax(1, 2, 3, 4)
                    row_norm(ln_first(0) + 1, xres)
                    next_amax(5)
                else:
                    next_amax(0, 1)
                    row_max(i, par)
                    next_amax(2)
                    prob_lo(i, par)
                    if full:
                        dve.wait_ge(s_xa, i * 16 + 48)
                        row_stats(ln_first(i), xa)
                    next_amax(3, 4, 5)
                if full:
                    part_max(i + 2)
                    scales(i + 2, par)
                    if not first:
                        row_norm(ln_first(i), xa)
                    for t in range(3):
                        lo(i + 2, par, t)
                if not first:
                    for n in range(NCH):
                        x1_piece(i, n)
                q = ln_first(i) + 1 if full else LN2_6
                if not first:
                    dve.wait_ge(s_x1, i * NCH + NCH)
                    row_stats(q, xres)
                if full:
                    for t in range(3, NT):
                        lo(i + 2, par, t)
                if not first:
                    row_norm(q, xres)

            unrolled(dve, step)

            def unpack(n, par, k):
                dve.wait_ge(s_w[par], k * 16 + 16)
                p = wraw[:, par, :].bitcast(U16).rearrange("p (g w h) -> p g w h", w=3, h=2)
                dve.tensor_scalar(unp[:, par, 1, :], p[:, :, 0, 0], 6, 63, ALU.logical_shift_right,
                                  ALU.bitwise_and).then_inc(s_u1, 1)
                for j, w in ((0, 0), (2, 1), (3, 2)):
                    dve.tensor_scalar(unp[:, par, j, :], p[:, :, w, 0], 63, 0x6400, ALU.bitwise_and, ALU.bitwise_or)
                dve.wait_ge(s_u1, n + 1)
                dve.tensor_scalar(unp[:, par, 1, :], unp[:, par, 1, :], 0x6400, None, ALU.bitwise_or).then_inc(s_u, 1)

            def w_out(n, par):
                dve.wait_ge(s_turned[1], w_use(n) + 1)
                dve.tensor_scalar(wT[:, par, HALF:CH, :], turn[1][:, :].bitcast(F16).rearrange("p (c n) -> p c n", n=P),
                                  -float(BIAS16), None, ALU.add).then_inc(s_evac[1], 1)

            for n in range(2):
                unpack(n, n, 0)
            row_max(LAST, LAST % 2)
            prob_lo(LAST, LAST % 2)
            w_out(0, 0)
            dve.wait_ge(s_bc, 32)
            dve.tensor_scalar(cB[0:R, :], cB[0:R, :], -1.0, 32.0, ALU.mult, ALU.add).then_inc(s_zp, 1)
            dve.wait_ge(s_zp, 1)
            dve.scalar_tensor_tensor(out=cB[0:R, :], in0=cB[0:R, :], scalar=tg[0:R, 2:3], in1=scB[0:R, :],
                                     op0=ALU.mult, op1=ALU.mult).then_inc(s_cB, 1)
            for n in range(NCH):
                x1_piece(LAST, n)
            dve.wait_ge(s_x1, NCH * B)
            row_stats(LN2_7, xres)
            w_out(1, 1)
            row_norm(LN2_7, xres)

            def rank_one(n):
                cols = bass.ds(n * P, P)
                for b in range(B):
                    last = dve.scalar_tensor_tensor(out=x1f[0:R, b, cols], in0=cB[0:R, cols], scalar=row_sum[0:R, b:b + 1],
                                                    in1=x1f[0:R, b, cols], op0=ALU.mult, op1=ALU.add)
                last.then_inc(s_r1, 1)

            def add_up(n, h):
                dve.wait_ge(s_yb, n * 2 + (h + 1))
                block_of = x1f[0:R, h * HB:(h + 1) * HB, bass.ds(n * P, P)]
                dve.tensor_tensor(block_of, BACK[h][0:R, :].rearrange("p (b n) -> p b n", b=HB), block_of,
                                  ALU.add).then_inc(s_add, 1)

            def w_step(n, par, k):
                first = isinstance(n, int) and n == 0
                if not first and (not isinstance(n, int) or n + 1 < NB):
                    w_out(n + 1, 1 - par)
                if not isinstance(n, int) or n + 2 < NB:
                    unpack(n + 2, par, k + 1)
                if first:
                    dve.wait_ge(s_x1in, 16 * (B - 1))
                    dve.wait_ge(s_xhi, 2 * B)
                    dve.wait_ge(s_cB, 1)
                if not first:
                    add_up(n - 1, 1)
                rank_one(n)
                dve.wait_ge(s_r1, n + 1)
                add_up(n, 0)

            w_steps(dve, w_step)
            add_up(NB - 1, 1)

        @block.tensor
        def _(pe):
            def free(k, u):
                if not (isinstance(u, int) and u == 0):
                    pe.wait_ge(s_evac[k], u)

            def turn_rows(u0, ready, b, columns, attended=lambda bank: None):
                pe.wait_ge(ready, b + 1)
                for m in range(2 * QU):
                    free(m % 2, u0 + m // 2)
                    if m < 2:
                        attended(m)
                    for k in range(QPB):
                        last = pe.transpose(turn[m % 2][:, k * R:(k + 1) * R], columns(m * QPB + k), ident[0:R, 0:R])
                    last.then_inc(s_turned[m % 2], 1)

            def q_cols(c):
                return rows[0:R, c * P:(c + 1) * P]

            def ffn_cols(c):
                j, gb = divmod(c, G4 // P)
                return rows[0:R, 4 * gb * P + j:4 * (gb + 1) * P:4]

            def score_group(b, par, g, u0, attended=lambda bank: None):
                pe.wait_ge(s_lo, b * NT + (3 * g + 3))
                for c in range(CH + 4):
                    if c < CH:
                        bank, use = chunk_use(u0, c)
                        free(bank, use)
                        if c < 4:
                            attended(bank)
                        for t in range(3):
                            n = ROWS[3 * g + t]
                            last = pe.transpose(turn[bank][:, t * P:t * P + n],
                                                pair_words[0:n, par * NT + 3 * g + t, c * P:(c + 1) * P],
                                                ident[0:n, 0:n])
                        last.then_inc(s_turned[bank], 1)
                    if c >= 4:
                        m = c - 4
                        bank, use = chunk_use(u0, m)
                        pe.wait_ge(s_evac[bank], use + 1)
                        for k, (a, e) in enumerate(((HI, HI), (HI, LO), (LO, HI))):
                            last = pe.matmul(S[0:R, par, g, 0:GW], qT16[:, par, m, :, a], ring16[:, m % RING, :, e],
                                             start=(m == 0 and k == 0), stop=(m == CH - 1 and k == 2))
                last.then_inc(s_scores, 1)

            def turn_probs(i, u):
                pe.wait_ge(s_plo, i + 1)
                for t in range(NT):
                    k = 2 + t // 3
                    if t % 3 == 0:
                        free(k, u)
                    n = ROWS[t]
                    last = pe.transpose(turn[k][0:n, (t % 3) * R:(t % 3 + 1) * R], prob[0:R, FIRST[t]:FIRST[t] + n],
                                        ident[0:R, 0:R])
                    if t % 3 == 2:
                        last.then_inc(s_turned[k], 1)

            def probs_turned(u):
                for k in (2, 3):
                    pe.wait_ge(s_evac[k], u + 1)

            def attend(i, par, low, high):
                for t in range(NT):
                    r = ROWS[t]
                    for n in (0, 1, 2, 3) if t else (2, 3, 0, 1):
                        if t == 0:
                            free(n, high if n > 1 else low)
                        for k, (a, e) in enumerate(((HI, HI), (HI, LO), (LO, HI))):
                            last = pe.matmul(turn[n][0:R, :], pT16[0:r, t, :, a],
                                             pair[0:r, par * NT + t, n * 512:(n + 1) * 512, e],
                                             start=(t == 0 and k == 0), stop=(t == NT - 1 and k == 2))
                        if t == NT - 1:
                            last.then_inc(s_pvn, 1)
                    if t < NT - 1:
                        last.then_inc(s_pvt, 1)

            def turn_weights(n, par):
                pe.wait_ge(s_u, n + 1)
                for c in range(CH):
                    if c % HALF == 0:
                        free(c // HALF, w_use(n))
                    j, gb = divmod(c, G4 // P)
                    last = pe.transpose(turn[c // HALF][:, :].bitcast(F16)[:, (c % HALF) * P:(c % HALF + 1) * P],
                                        unp[:, par, j, gb * P:(gb + 1) * P].bitcast(F16), ident16[:, :])
                    if c % HALF == HALF - 1:
                        last.then_inc(s_turned[c // HALF], 1)

            pe.wait_ge(s_id, 2)
            u = Uses(0, 0)
            turn_rows(u.take(QU), s_qrows, 0, q_cols)
            score_group(0, 0, 0, u.group())
            score_group(0, 0, 1, u.group())
            probs = u.take_high(1)
            turn_probs(0, probs)
            probs_turned(probs)
            attend(0, 0, u.take(0), u.take_high(0))

            def first_attended(bank):
                pe.wait_ge(s_x1, bank + 1)

            turn_rows(u.take(QU), s_qrows, 1, q_cols, first_attended)
            score_group(1, 1, 0, u.group(), first_attended)

            def step(i, par, full):
                u = step_uses(i)
                if not (isinstance(i, int) and i == 0):
                    attend(i, par, u.take(0), u.take_high(0))

                def attended(bank):
                    pe.wait_ge(s_x1, i * NCH + (bank + 1))

                if full:
                    turn_rows(u.take(QU), s_qrows, i + 2, q_cols, attended)
                score_group(i + 1, 1 - par, 1, u.group(), attended)
                if full:
                    score_group(i + 2, par, 0, u.group())
                probs = u.take_high(1)
                if full:
                    turn_probs(i + 1, probs)
                turn_rows(u.take(QU), s_frows, i, ffn_cols)
                if not full:
                    turn_probs(i + 1, probs)
                    turn_weights(0, 0)
                probs_turned(probs)

            unrolled(pe, step)

            def multiply(n, par, h):
                if not (isinstance(n, int) and n == 0):
                    pe.wait_ge(s_yev, n * 2 + (h - 1))
                for c in range(CH):
                    for k in (HI, LO):
                        last = pe.matmul(Y[h][:, 0:HR], wT[:, par, c, :], xTv[:, h * HB:(h + 1) * HB, c, :, k],
                                         start=(c == 0 and k == HI), stop=(c == CH - 1 and k == LO))
                last.then_inc(s_y, 1)

            def turn_back(n, h):
                pe.wait_ge(s_yev, n * 2 + (h + 1))
                if not (isinstance(n, int) and n == 0):
                    pe.wait_ge(s_add, n * 2 + (h - 1))
                for b in range(HB):
                    last = pe.transpose(BACK[h][0:R, b * P:(b + 1) * P], yT[:, h, b * R:(b + 1) * R], ident[:, :])
                last.then_inc(s_yb, 1)

            attend(LAST, LAST % 2, W_USE + 1, PRO[1] + LAST * STEP[1] - GU)
            pe.wait_ge(s_x1, LAST * NCH + 2)
            turn_weights(1, 1)
            for q in range(2):
                pe.wait_ge(s_evac[q], w_use(0) + 1)
            pe.wait_ge(s_xTin, 16 * (B - 2))
            multiply(0, 0, 0)
            turn_rows(C_LAST, s_frows, LAST, ffn_cols)
            pe.wait_ge(s_xTin, 16 * (B - 1))
            pe.wait_ge(s_x1, NCH * B)

            def w_step(n, par, k):
                if isinstance(n, int) and n == 0:
                    for q in range(2):
                        pe.wait_ge(s_evac[q], C_LAST + QU)
                    multiply(0, 0, 1)
                    turn_back(0, 0)
                    return
                for q in range(2):
                    pe.wait_ge(s_evac[q], w_use(n) + 1)
                if not isinstance(n, int) or n + 1 < NB:
                    turn_weights(n + 1, 1 - par)
                multiply(n, par, 0)
                turn_back(n - 1, 1)
                multiply(n, par, 1)
                turn_back(n, 0)

            w_steps(pe, w_step)
            turn_back(NB - 1, 1)


_INS = ["x", "ctx_4096", "g_xattn", "g_ffn", "L0_ffn_qweight", "L0_ffn_weight_scale", "L0_ffn_weight_zero_point", "L0_ffn_bias"]


def kernel(**inputs):
    import numpy as np
    import concourse.bacc as bacc
    from concourse.bass_utils import run_bass_kernel_spmd

    nc = bacc.Bacc("TRN2", target_bir_lowering=False, num_devices=1)
    arrays, args = {}, []
    for name in _INS:
        a = np.ascontiguousarray(inputs[name])
        arrays[f"in_{name}"] = a
        args.append(nc.dram_tensor(f"in_{name}", a.shape, mybir.dt.from_np(a.dtype), kind="ExternalInput").ap())
    shape = np.asarray(inputs["x"]).shape
    args.append(nc.dram_tensor("out_y", shape, F32, kind="ExternalOutput").ap())
    flamingo_block(nc, *args)
    r = run_bass_kernel_spmd(nc, [arrays], core_ids=[0])
    return r.results[0]["out_y"]
```
